# Optimizing a Trainium2 kernel written in Bass

```python
import numpy as np
import jax
import jax.numpy as jnp

def _softmax(x, axis=-1):
    return jax.nn.softmax(x, axis=axis)

def _gelu(x):
    return jax.nn.gelu(x, approximate=True)

def _silu(x):
    return jax.nn.silu(x)

def _sigmoid(x):
    return jax.nn.sigmoid(x)

def _layernorm(x, axis=-1, eps=1e-05):
    m = jnp.mean(x, axis=axis, keepdims=True)
    v = jnp.var(x, axis=axis, keepdims=True)
    return (x - m) / jnp.sqrt(v + eps)

def _scatter_add(tgt, idx, src, axis=0):
    return tgt.at[idx].add(src)

def _segment_sum(src, seg, n):
    return jax.ops.segment_sum(src, seg, n)
kernel_name = 'mk_gnn_preln_d1_gnn_r8_429d09'

def setup_inputs(seed: int=0):
    np.random.seed(seed)
    _w = jnp.asarray

    def _rec_inputs():
        import jax
        import jax.numpy as jnp
        _gk = jax.random.key(seed)
        x = -8.776e-05 + 1 * jax.random.normal(jax.random.fold_in(_gk, 1), (6250, 256), jnp.float32)
        _s = jax.random.randint(jax.random.fold_in(_gk, 2), (100000,), 0, 6250, jnp.int32)
        _d = jax.random.randint(jax.random.fold_in(_gk, 3), (100000,), 0, 6250, jnp.int32)
        _loop = jnp.arange(6250, dtype=jnp.int32)
        src = jnp.concatenate([_s, _d, _loop])
        dst = jnp.concatenate([_d, _s, _loop])
        _o = jnp.argsort(dst, stable=True)
        src = src[_o]
        dst = dst[_o]
        edge_type_8 = jax.random.randint(jax.random.fold_in(_gk, 12), (206250,), 0, 8, jnp.int32)
        return (x, src, dst, edge_type_8)
    x, src, dst, edge_type_8 = _rec_inputs()

    def _L0_gnn_setup():
        import jax, jax.numpy as jnp
        import numpy as np
        N_NODES = 2500
        N_EDGES = 80000
        D = 256
        N_RELS = 8
        N_BASES = 4
        LN_EPS = 1e-05
        key = jax.random.key(seed)
        ks = jax.random.split(key, 8)
        node_feats = jax.random.normal(ks[0], (N_NODES, D), dtype=jnp.float32)
        src = jax.random.randint(ks[1], (N_EDGES,), 0, N_NODES, dtype=jnp.int32)
        dst = jax.random.randint(ks[2], (N_EDGES,), 0, N_NODES, dtype=jnp.int32)
        edge_types = jax.random.randint(ks[3], (N_EDGES,), 0, N_RELS, dtype=jnp.int32)
        basis = jax.random.normal(ks[4], (N_BASES, D, D), dtype=jnp.float32) * (1.0 / np.sqrt(D))
        comp = jax.random.normal(ks[5], (N_RELS, N_BASES), dtype=jnp.float32) * (1.0 / np.sqrt(N_BASES))
        loop_w = jax.random.normal(ks[6], (D, D), dtype=jnp.float32) * (1.0 / np.sqrt(D))
        h_bias = jnp.zeros((D,), dtype=jnp.float32)
        ln_gamma = jnp.ones((D,), dtype=jnp.float32)
        ln_beta = jnp.zeros((D,), dtype=jnp.float32)
        return {'node_feats': node_feats, 'src': src, 'dst': dst, 'edge_types': edge_types, 'basis': basis, 'comp': comp, 'loop_w': loop_w, 'h_bias': h_bias, 'ln_gamma': ln_gamma, 'ln_beta': ln_beta}
    _L0_gnn_all = _L0_gnn_setup()
    _L0_gnn_in = {k: v for k, v in _L0_gnn_all.items() if k in ('basis', 'comp', 'loop_w', 'h_bias', 'ln_gamma', 'ln_beta')}
    del _L0_gnn_all
    return {'x': x, 'src': src, 'dst': dst, 'edge_type_8': edge_type_8, 'L0_gnn_basis': _L0_gnn_in['basis'], 'L0_gnn_comp': _L0_gnn_in['comp'], 'L0_gnn_loop_w': _L0_gnn_in['loop_w'], 'L0_gnn_h_bias': _L0_gnn_in['h_bias'], 'L0_gnn_ln_gamma': _L0_gnn_in['ln_gamma'], 'L0_gnn_ln_beta': _L0_gnn_in['ln_beta']}

def reference(x, src, dst, edge_type_8, L0_gnn_basis, L0_gnn_comp, L0_gnn_loop_w, L0_gnn_h_bias, L0_gnn_ln_gamma, L0_gnn_ln_beta):
    import jax
    import jax.numpy as jnp

    def _L0_gnn_ref(node_feats, src, dst, edge_types, basis, comp, loop_w, h_bias, ln_gamma, ln_beta):
        import jax, jax.numpy as jnp
        import numpy as np
        N_NODES = 2500
        N_EDGES = 80000
        D = 256
        N_RELS = 8
        N_BASES = 4
        LN_EPS = 1e-05
        W = jnp.einsum('rb,bio->rio', comp, basis)
        h_all = jnp.einsum('ni,rio->nro', node_feats, W)
        msgs = h_all[src, edge_types]
        agg = jax.ops.segment_sum(msgs, dst, num_segments=node_feats.shape[0])
        rgcn_out = agg + node_feats @ loop_w + h_bias
        h = jax.nn.gelu(rgcn_out + node_feats, approximate=False)
        mu = jnp.mean(h, axis=-1, keepdims=True)
        var = jnp.mean(jnp.square(h - mu), axis=-1, keepdims=True)
        return (h - mu) * jax.lax.rsqrt(var + LN_EPS) * ln_gamma + ln_beta
    h = jnp.maximum(_layernorm(x, axis=-1), 0.0)
    x = x + _L0_gnn_ref(h, src, dst, edge_type_8, L0_gnn_basis, L0_gnn_comp, L0_gnn_loop_w, L0_gnn_h_bias, L0_gnn_ln_gamma, L0_gnn_ln_beta)
    return x

_drawn_inputs = setup_inputs


def setup_inputs(seed=0):
    import zlib

    import numpy as np

    out = dict(_drawn_inputs(seed))
    spreads = {'L0_gnn_h_bias': (0.0, 0.567), 'L0_gnn_ln_gamma': (1.0, 0.2), 'L0_gnn_ln_beta': (0.0, 0.1)}
    factors = {}
    for name, (base, spread) in spreads.items():
        noise = np.random.default_rng([zlib.crc32(name.encode()), seed]).standard_normal(out[name].shape)
        drawn = base * np.exp(spread * noise) if base else spread * noise
        out[name] = jnp.asarray(drawn.astype(out[name].dtype))
    for name, factor in factors.items():
        out[name] = (out[name] * factor).astype(out[name].dtype)
    return out
```

```python
from contextlib import ExitStack

import numpy as np

import concourse.bass as bass
from concourse import mybir

F32 = mybir.dt.float32
I32 = mybir.dt.int32
ALU = mybir.AluOpType
ACT = mybir.ActivationFunctionType
AX = mybir.AxisListType.X

P = 128
EPS = 1e-5


def build_rgcn(nc, x, src, dst, etype, basis, comp, loop_w, h_bias, ln_gamma, ln_beta, out):
    N, D = x.shape
    E = src.shape[0]
    NB = basis.shape[0]
    NR = comp.shape[0]
    HALVES = D // P
    KB = HALVES * NB

    GT = 6
    SG = 11
    WIN = 32
    STEP = 2 * P
    ST = SG * GT
    NG = -(-E // (GT * P))
    NT = NG * GT
    S_LAST = N // STEP
    LAST_G = NG - S_LAST * SG
    assert 0 < LAST_G <= SG
    AW = 2 * STEP + 2 * WIN
    SETTLED = 4
    EB = -(-NT // P)
    FULL_T, REST_E = E // P, E % P
    MAIN_T = (FULL_T // P) * P
    REST_T = FULL_T - MAIN_T

    ROWS = N // P
    REST_N = N - ROWS * P
    CR = 8
    NCHUNK = ROWS // CR
    XS = 3
    assert NCHUNK % XS == 0 and ROWS % CR == 0
    NPAIR = N // STEP
    assert N - NPAIR * STEP == REST_N
    AGG_ROWS = -(-(N + P) // P) * P
    DB = NB * D

    h_table = nc.dram_tensor("h_table", [N, D], F32, kind="Internal").ap()
    agg_table = nc.dram_tensor("agg_table", [AGG_ROWS, DB], F32, kind="Internal").ap()

    ctx = ExitStack()
    with ctx:
        def sb(name, shape, dt=F32):
            return ctx.enter_context(nc.sbuf_tensor(name, shape, dt))

        def ps(name, shape):
            return ctx.enter_context(nc.psum_tensor(name, shape, F32))

        def sem(name):
            return ctx.enter_context(nc.semaphore(name))

        ident = sb("ident", [P, P])
        ones = sb("ones", [P, P])
        below = sb("below", [P, P])
        iota_i = sb("iota_i", [P, (S_LAST + 1) * SG], I32)
        iota_win = sb("iota_win", [P, WIN])
        iota_rel = sb("iota_rel", [P, NR])
        waste_i = sb("waste_i", [P, 1], I32)
        waste = sb("waste", [P, 1])
        step_base = sb("step_base", [P, (S_LAST + 1) * SG])
        least = sb("least", [P, S_LAST + 1, SG])
        basis_sb = sb("basis_sb", [P, NB, HALVES, D])
        loop_sb = sb("loop_sb", [P, HALVES, D])
        comp_sb = sb("comp_sb", [P, NR, NB])
        bias_sb = sb("bias_sb", [P, D])
        gamma_sb = sb("gamma_sb", [P, D])
        beta_sb = sb("beta_sb", [P, D])

        raw = sb("raw", [P, EB, P], I32)
        rawf = sb("rawf", [P, EB, P])
        srcT = sb("srcT", [P, EB * P])
        dstT = sb("dstT", [P, EB * P])
        typT = sb("typT", [P, EB * P])
        dloc = sb("dloc", [P, NG, GT])
        room = sb("room", [P, NG])
        offs = sb("offs", [P, NG])
        offs_i = sb("offs_i", [1, NG], I32)
        lim = sb("lim", [P, 4])
        okay = sb("okay", [P, 4])
        flag_i = sb("flag_i", [1, 1], I32)

        xc = [sb(f"xc{i}", [P, CR, D]) for i in range(XS)]
        xr = sb("xr", [REST_N, D])
        bn = sb("bn", [P, CR, 6])
        mv = [sb(f"mv{i}", [P, CR, 2]) for i in range(2)]
        eps_sb = sb("eps_sb", [P, 1])
        rstd = [sb(f"rstd{i}", [P, CR]) for i in range(XS)]
        nmr = [sb(f"nmr{i}", [P, CR]) for i in range(XS)]

        src_now = sb("src_now", [P, ST], I32)
        gath = sb("gath", [P, SG, GT, D])
        typ_is = sb("typ_is", [P, ST, NR])
        typ_comp = sb("typ_comp", [P, ST, NB, NR])
        coef = sb("coef", [P, ST, NB])
        here = sb("here", [P, GT, WIN])
        MS = 3
        M = sb("M", [P, MS, GT, NB, WIN])
        acc = sb("acc", [P, KB, AW])

        x_nt = [sb(f"x_nt{q}", [P, D]) for q in range(2)]
        h_nt = [sb(f"h_nt{q}", [P, D]) for q in range(2)]
        hT_nt = [sb(f"hT_nt{q}", [P, HALVES, P]) for q in range(2)]
        z_nt = [sb(f"z_nt{q}", [P, D]) for q in range(2)]
        bn_nt = [sb(f"bn_nt{q}", [P, 6]) for q in range(2)]
        mv_nt = [sb(f"mv_nt{q}", [P, 2]) for q in range(2)]
        rstd_nt = [sb(f"rstd_nt{q}", [P, 1]) for q in range(2)]
        nmr_nt = [sb(f"nmr_nt{q}", [P, 1]) for q in range(2)]
        y_nt = [sb(f"y_nt{q}", [P, D]) for q in range(2)]

        g_src = src_now[:, 0:1]
        g_dst_i = src_now[:, 1:2]
        g_dst = sb("g_dst", [P, 1])
        g_first = sb("g_first", [P, 2])
        g_coef = sb("g_coef", [P, NB])
        g_tc = typ_comp[:, 0, :, :]
        g_ti = typ_is[:, 0, :]
        g_rows = gath[:, 0, 0, :]
        g_wide = gath[:, 1, 0, 0:P]
        g_same = gath[:, 1, 1, 0:P]
        g_prev = gath[:, 1, 2, 0:P]
        g_M = gath[:, 2, 0:2, :].rearrange("p t (a e) -> p (t a) e", a=2)
        g_sums = gath[:, 3, 0:NB, :].rearrange("p t d -> p (t d)")
        g_zero = gath[:, 4, 0:NB, :].rearrange("p t d -> p (t d)")
        agg_nt = [gath[:, 5 + q, 0:NB, :].rearrange("p t d -> p (t d)") for q in range(2)]
        aggT_nt = [gath[:, 7 + q, 0:NB, :].rearrange("p t d -> p (t d)") for q in range(2)]

        p_sum = [ps(f"p_sum{i}", [P, 512]) for i in range(MS)]
        p_first = ps("p_first", [P, 512])
        p_out = [ps(f"p_out{q}", [P, 512]) for q in range(2)]
        p_wide = ps("p_wide", [P, 1024])

        s_const = sem("s_const")
        s_par = sem("s_par")
        s_raw = [sem(f"s_raw{n}") for n in range(3)]
        s_pad = sem("s_pad")
        s_flt = sem("s_flt")
        s_tr = sem("s_tr")
        s_trc = sem("s_trc")
        s_x = [sem(f"s_x{i}") for i in range(XS)]
        s_xr = sem("s_xr")
        s_bn = sem("s_bn")
        s_eps = sem("s_eps")
        s_std = sem("s_std")
        s_h = sem("s_h")
        s_hd = [sem(f"s_hd{i}") for i in range(XS)]
        s_hr = sem("s_hr")
        s_first = sem("s_first")
        s_chk = sem("s_chk")
        s_cnt = sem("s_cnt")
        s_flag = sem("s_flag")
        held = sem("held")

        s_stage = sem("s_stage")
        s_gath = [sem(f"s_gath{j}") for j in range(SG)]
        s_coef = sem("s_coef")
        s_here = sem("s_here")
        s_M = sem("s_M")
        s_agg = sem("s_agg")
        s_flush = sem("s_flush")
        s_shift = sem("s_shift")

        s_ld = [sem(f"s_ld{q}") for q in range(2)]
        s_hT = [sem(f"s_hT{q}") for q in range(2)]
        s_hTc = [sem(f"s_hTc{q}") for q in range(2)]
        s_mm = [sem(f"s_mm{q}") for q in range(2)]
        s_z = [sem(f"s_z{q}") for q in range(2)]
        s_gelu = [sem(f"s_gelu{q}") for q in range(2)]
        s_nrm = [sem(f"s_nrm{q}") for q in range(2)]
        s_aff = [sem(f"s_aff{q}") for q in range(2)]
        s_res = [sem(f"s_res{q}") for q in range(2)]
        s_out = [sem(f"s_out{q}") for q in range(2)]

        g_zeroed = sem("g_zeroed")
        g_clear = sem("g_clear")
        g_staged = sem("g_staged")
        g_gath = sem("g_gath")
        g_wid = sem("g_wid")
        g_tr = sem("g_tr")
        g_mk = sem("g_mk")
        g_mm = sem("g_mm")
        g_copied = sem("g_copied")
        g_added = sem("g_added")
        g_ld = [sem(f"g_ld{q}") for q in range(2)]
        g_aT = sem("g_aT")
        g_aTc = sem("g_aTc")

        block = ctx.enter_context(nc.Block())

        def hold(eng, semaphore, value):
            eng.wait_ge(semaphore, value)
            eng.sem_inc(held, 1)

        def bn_steps(i):
            return 0 if i == 0 else 4 * i - 2

        lists = (src, dst, etype)
        pads = (0, N - 1, NR)

        x_rows = x[0:ROWS * P, :].rearrange("(p r) d -> p r d", p=P)
        h_rows = h_table[0:ROWS * P, :].rearrange("(p r) d -> p r d", p=P)

        G_BATCH = 4
        tr_batches = [(n, b, min(G_BATCH, EB - b)) for n in range(3) for b in range(0, EB, G_BATCH)]
        NBATCH = len(tr_batches) // 3
        listT = (srcT, dstT, typT)

        def tr_bank(i):
            return (p_wide[:, 0:512], p_wide[:, 512:1024], p_sum[0][:, :], p_sum[1][:, :])[i % 4]


        def sp_load_nt(sp, q, row, rows):
            sp.dma_start(x_nt[q][0:rows, :], x[bass.ds(row, rows), :]).then_inc(s_ld[q], 16)
            sp.dma_start(h_nt[q][0:rows, :], h_table[bass.ds(row, rows), :]).then_inc(s_ld[q], 16)

        def sp_store_nt(sp, q, k, row, rows):
            sp.wait_ge(s_res[q], k + 1)
            sp.dma_start(out[bass.ds(row, rows), :], y_nt[q][0:rows, :]).then_inc(s_out[q], 16)

        def sp_node_tiles(sp, k, row, sizes, sums=None):
            for q, rows in enumerate(sizes):
                if sums is not None:
                    sums(q, row + q * P, rows)
                sp_load_nt(sp, q, row + q * P, rows)
            for q, rows in enumerate(sizes):
                sp_store_nt(sp, q, k, row + q * P, rows)
            for q, rows in enumerate(sizes):
                hold(sp, s_out[q], k * 16 + 16)

        @block.sync
        def _(sp):
            def load_list(n):
                a = lists[n]
                sp.dma_start(raw[:, 0:MAIN_T // P, :],
                             a[0:MAIN_T * P].rearrange("(b t e) -> t b e", t=P, e=P)).then_inc(s_raw[n], 16)
                sp.wait_ge(s_pad, n + 1)
                if REST_T:
                    sp.dma_start(raw[0:REST_T, EB - 1, :],
                                 a[MAIN_T * P:FULL_T * P].rearrange("(t e) -> t e", e=P)).then_inc(s_raw[n], 16)
                if REST_E:
                    sp.dma_start(raw[REST_T:REST_T + 1, EB - 1, 0:REST_E],
                                 a[FULL_T * P:E].rearrange("(t e) -> t e", t=1)).then_inc(s_raw[n], 16)

            sp.dma_start(xr[:, :], x[ROWS * P:N, :]).then_inc(s_xr, 16)
            for i in range(XS):
                sp.dma_start(xc[i][:, :, :], x_rows[:, i * CR:(i + 1) * CR, :]).then_inc(s_x[i], 16)
            load_list(0)
            sp.wait_ge(s_flt, 1)
            load_list(1)
            for i in range(XS, NCHUNK):
                sp.wait_ge(s_hd[i % XS], 16 * (i // XS))
                sp.dma_start(xc[i % XS][:, :, :],
                             x_rows[:, i * CR:(i + 1) * CR, :]).then_inc(s_x[i % XS], 16)
            sp.wait_ge(s_flt, 2)
            load_list(2)
            for to, what in ((basis_sb[:, :, :, :], basis.rearrange("b (h p) o -> p b h o", p=P)),
                             (loop_sb[:, :, :], loop_w.rearrange("(h p) o -> p h o", p=P)),
                             (comp_sb[:, :, :].rearrange("p r b -> p (r b)"),
                              comp.rearrange("r b -> (r b)").partition_broadcast(P)),
                             (bias_sb[:, :], h_bias.partition_broadcast(P)),
                             (gamma_sb[:, :], ln_gamma.partition_broadcast(P)),
                             (beta_sb[:, :], ln_beta.partition_broadcast(P))):
                sp.dma_start(to, what).then_inc(s_par, 16)

            sp.wait_ge(s_flag, 1)
            windows = sp.value_load(flag_i[0:1, 0:1], min_val=0, max_val=1)
            for i in range(XS):
                sp.wait_ge(s_hd[i], 16 * (NCHUNK // XS))
            sp.wait_ge(s_hr, 16)
            with sp.If(windows):
                with sp.Fori(1, S_LAST) as s:
                    sp_node_tiles(sp, s - 1, s * STEP - STEP, (P, P))
                sp_node_tiles(sp, S_LAST - 1, (S_LAST - 1) * STEP, (P, P))
                sp_node_tiles(sp, NPAIR, NPAIR * STEP, (REST_N,))
            with sp.Else():
                sp.wait_ge(g_zeroed, 1)
                sp.dma_start(agg_table.rearrange("(j p) c -> p j c", p=P),
                             g_zero.unsqueeze(1).to_broadcast([P, AGG_ROWS // P, DB])).then_inc(g_clear, 16)
                sp.wait_ge(g_added, 16 * NT)

                def load_sums(q, row, rows):
                    sp.dma_start(agg_nt[q][0:rows, :], agg_table[bass.ds(row, rows), :]).then_inc(g_ld[q], 16)

                with sp.Fori(0, NPAIR) as i:
                    sp_node_tiles(sp, i, i * STEP, (P, P), load_sums)
                sp_node_tiles(sp, NPAIR, NPAIR * STEP, (REST_N,), load_sums)
            sp.wait_ge(s_out[0], 16 * (NPAIR + 1))
            sp.wait_ge(s_out[1], 16 * NPAIR)


        @block.gpsimd
        def _(pool):
            pool.memset(ident[:, :], 0.0).then_inc(s_const, 1)
            pool.memset(ones[:, :], 1.0).then_inc(s_const, 1)
            pool.wait_ge(s_const, 2)
            pool.affine_select(out=ident[:, :], in_=ident[:, :], compare_op=ALU.not_equal, fill=1.0,
                               base=0, pattern=[[-1, P]], channel_multiplier=1).then_inc(s_const, 1)
            pool.memset(eps_sb[:, :], EPS).then_inc(s_eps, 1)
            for n in range(3):
                if n:
                    pool.wait_ge(s_flt, n)
                pool.memset(raw[:, EB - 1, :], pads[n]).then_inc(s_pad, 1)
                if n == 0:
                    pool.affine_select(out=below[:, :], in_=ones[:, :], compare_op=ALU.is_gt, fill=0.0,
                                       base=0, pattern=[[-1, P]], channel_multiplier=1)
                    pool.iota(iota_i[:, 0:WIN], pattern=[[1, WIN]], base=0, channel_multiplier=0)
                    pool.iota(waste_i[:, :], pattern=[[0, 1]], base=N, channel_multiplier=1).then_inc(s_const, 1)
                    pool.wait_ge(s_const, 4)
                    pool.tensor_copy(iota_win[:, :], iota_i[:, 0:WIN])
                    pool.tensor_copy(iota_rel[:, :], iota_i[:, 0:NR])
                    pool.tensor_copy(waste[:, :], waste_i[:, :]).then_inc(s_const, 1)
                    pool.wait_ge(s_const, 5)
                    pool.iota(iota_i[:, :], pattern=[[-STEP, S_LAST + 1], [0, SG]], base=STEP,
                              channel_multiplier=0)
                    pool.memset(least[:, :, :], 0.0).then_inc(s_const, 1)
                    pool.wait_ge(s_const, 6)
                    pool.tensor_copy(step_base[:, :], iota_i[:, :])
                    pool.memset(least[:, 0:S_LAST, SETTLED:SG], float(STEP)).then_inc(s_const, 1)
                pool.wait_ge(s_raw[n], 16 * (1 + bool(REST_T) + bool(REST_E)))
                if n:
                    pool.wait_ge(s_tr, NBATCH * n)
                pool.tensor_copy(rawf[:, :, :], raw[:, :, :]).then_inc(s_flt, 1)

            pool.wait_ge(s_flag, 1)
            windows = pool.value_load(flag_i[0:1, 0:1], min_val=0, max_val=1)
            for i in range(XS):
                pool.wait_ge(s_hd[i], 16 * (NCHUNK // XS))
            pool.wait_ge(s_hr, 16)

            def gather(to, index, semaphore):
                pool.indirect_dma_start(to, None, h_table,
                                        bass.IndirectOffsetOnAxis(ap=index, axis=0)).then_inc(semaphore, 16)

            def superstep(s, groups):
                first = isinstance(s, int) and s == 0
                for j in range(groups):
                    if not first:
                        hold(pool, s_agg, (s - 1) * SG + j + 1)
                    if j == 0 or j == GT:
                        hold(pool, s_stage, s * 2 + (1 if j == 0 else 2))
                    for t in range(GT):
                        gather(gath[:, j, t, :], src_now[:, j * GT + t:j * GT + t + 1], s_gath[j])

            with pool.If(windows):
                superstep(0, SG)
                with pool.Fori(1, S_LAST) as s:
                    superstep(s, SG)
                superstep(S_LAST, LAST_G)
            with pool.Else():
                pool.wait_ge(g_clear, 16)
                with pool.Fori(0, NT) as k:
                    hold(pool, g_staged, k + 1)
                    gather(g_rows, g_src, g_gath)
                    hold(pool, g_copied, k + 1)
                    pool.indirect_dma_start(
                        agg_table, bass.IndirectOffsetOnAxis(ap=g_dst_i, axis=0), g_sums, None,
                        compute_op=ALU.add).then_inc(g_added, 16)


        def pe_transpose_h(pe, q, k, rows):
            hold(pe, s_ld[q], (k + 1) * 32)
            for half in range(HALVES):
                last = nc.tensor.transpose(p_out[q][:, D + half * P:D + half * P + rows],
                                           h_nt[q][0:rows, half * P:(half + 1) * P], ident[0:rows, 0:rows])
            last.then_inc(s_hT[q], 1)

        def pe_node_tile(pe, q, k, rows, sums):
            hold(pe, s_hTc[q], k + 1)
            for half in range(HALVES):
                nc.tensor.matmul(p_out[q][0:rows, 0:D], hT_nt[q][:, half, 0:rows], loop_sb[:, half, :],
                                 start=(half == 0), stop=False)
            for half in range(HALVES):
                for b in range(NB):
                    last = nc.tensor.matmul(p_out[q][0:rows, 0:D], sums(half, b), basis_sb[:, b, half, :],
                                            start=False, stop=(half == HALVES - 1 and b == NB - 1))
            last.then_inc(s_mm[q], 1)

        @block.tensor
        def _(pe):
            pe.wait_ge(s_const, 3)
            for i, (n, b0, nb) in enumerate(tr_batches):
                if b0 == 0:
                    pe.wait_ge(s_flt, n + 1)
                if i >= 4:
                    pe.wait_ge(s_trc, i - 3)
                for b in range(nb):
                    last = nc.tensor.transpose(tr_bank(i)[:, b * P:(b + 1) * P], rawf[:, b0 + b, :], ident[:, :])
                last.then_inc(s_tr, 1)
                if i + 1 == 2 * NBATCH:
                    pe.wait_ge(s_trc, 2 * NBATCH)
                    nc.tensor.matmul(p_first[:, 0:NG], ones[0:1, :],
                                     dstT[0:1, 0:NT].rearrange("p (g t) -> p g t", t=GT)[:, :, 0],
                                     start=True, stop=True).then_inc(s_first, 1)
            pe.wait_ge(s_chk, 8)
            nc.tensor.matmul(p_out[0][0:1, 0:1], okay[:, 0:1], ones[:, 0:1], start=True, stop=True).then_inc(s_cnt, 1)

            pe.wait_ge(s_flag, 1)
            windows = pe.value_load(flag_i[0:1, 0:1], min_val=0, max_val=1)
            pe.wait_ge(s_par, 16 * 6)

            def acc_tile(at, rows):
                return lambda half, b: acc[:, half * NB + b, at:at + rows]

            def group(s, j):
                g = s * SG + j
                hold(pe, s_gath[j], (s + 1) * (16 * GT))
                free = g - 1 if j < 2 else g - 2
                if not (isinstance(s, int) and s == 0 and j < MS):
                    hold(pe, s_flush, free)
                pe.wait_ge(s_M, g + 1)
                for half in range(HALVES):
                    for t in range(GT):
                        last = nc.tensor.matmul(p_sum[j % MS][:, half * P:(half + 1) * P],
                                                gath[:, j, t, half * P:(half + 1) * P],
                                                M[:, j % MS, t, :, :].rearrange("p b w -> p (b w)"),
                                                start=(t == 0), stop=(t == GT - 1))
                last.then_inc(s_agg, 1)

            def superstep(s, groups):
                first = isinstance(s, int) and s == 0
                for j in range(groups):
                    group(s, j)
                    if first or groups < SG:
                        continue
                    for q, at in ((0, SETTLED), (1, SETTLED + 3)):
                        if j == at:
                            pe_transpose_h(pe, q, s - 1, P)
                        if j == at + 1:
                            hold(pe, s_flush, s * SG + SETTLED)
                            pe_node_tile(pe, q, s - 1, P, acc_tile(q * P, P))

            with pe.If(windows):
                superstep(0, SG)
                with pe.Fori(1, S_LAST) as s:
                    superstep(s, SG)
                superstep(S_LAST, LAST_G)
                pe.wait_ge(s_flush, NG)
                for q in range(2):
                    pe_transpose_h(pe, q, S_LAST - 1, P)
                for q in range(2):
                    pe_node_tile(pe, q, S_LAST - 1, P, acc_tile(q * P, P))
                pe_transpose_h(pe, 0, NPAIR, REST_N)
                pe_node_tile(pe, 0, NPAIR, REST_N, acc_tile(STEP, REST_N))
            with pe.Else():
                with pe.Fori(0, NT) as k:
                    pe.wait_ge(g_wid, k + 1)
                    nc.tensor.transpose(p_sum[0][:, 0:P], g_wide, ident[:, :]).then_inc(g_tr, 1)
                    hold(pe, g_gath, k * 16 + 16)
                    pe.wait_ge(g_mk, k * 9 + 9)
                    for b in range(NB):
                        last = nc.tensor.matmul(p_wide[:, b * D:(b + 1) * D], g_M[:, b, :], g_rows,
                                                start=True, stop=True)
                    last.then_inc(g_mm, 1)

                def node_tile(q, k, n, rows):
                    pe_transpose_h(pe, q, k, rows)
                    hold(pe, g_ld[q], k * 16 + 16)
                    for c in range(KB):
                        last = nc.tensor.transpose(p_wide[:, c * P:c * P + rows],
                                                   agg_nt[q][0:rows, c * P:(c + 1) * P], ident[0:rows, 0:rows])
                    last.then_inc(g_aT, 1)
                    hold(pe, g_aTc, n + 1)
                    pe_node_tile(pe, q, k, rows,
                                 lambda half, b: aggT_nt[q][:, (b * HALVES + half) * P:(b * HALVES + half) * P + rows])

                pe.wait_ge(g_copied, NT)
                with pe.Fori(0, NPAIR) as i:
                    for q in range(2):
                        node_tile(q, i, i * 2 + q, P)
                node_tile(0, NPAIR, 2 * NPAIR, REST_N)


        def act_copy_h(act, q, k, rows):
            act.wait_ge(s_hT[q], k + 1)
            nc.scalar.copy(hT_nt[q][:, :, 0:rows],
                           p_out[q][:, D:2 * D].rearrange("p (h r) -> p h r", h=HALVES)[:, :, 0:rows]
                           ).then_inc(s_hTc[q], 1)

        def act_gelu(act, q, k, rows):
            act.wait_ge(s_z[q], k * 2 + 2)
            nc.scalar.activation(z_nt[q][0:rows, :], z_nt[q][0:rows, :], ACT.Gelu).then_inc(s_gelu[q], 1)
            act.wait_ge(s_nrm[q], k * 5 + 2)
            nc.scalar.activation(rstd_nt[q][0:rows, :], mv_nt[q][0:rows, 1:2], ACT.Sqrt,
                                 bias=eps_sb[0:rows, :]).then_inc(s_nrm[q], 1)

        def act_affine(act, q, k, rows):
            act.wait_ge(s_nrm[q], k * 5 + 5)
            nc.scalar.activation(y_nt[q][0:rows, :], z_nt[q][0:rows, :], ACT.Identity,
                                 bias=nmr_nt[q][0:rows, :], scale=rstd_nt[q][0:rows, :]).then_inc(s_aff[q], 1)

        @block.scalar
        def _(act):
            def relu_chunk(buf, rows, r, slot, done):
                for i in range(r):
                    last = nc.scalar.activation(buf[0:rows, i, :], buf[0:rows, i, :], ACT.Relu,
                                                bias=nmr[slot][0:rows, i:i + 1], scale=rstd[slot][0:rows, i:i + 1])
                last.then_inc(s_h, 1)
                act.wait_ge(s_h, done)

            def std_chunk(i):
                rows, r = (REST_N, 1) if i == 0 else (P, CR)
                act.wait_ge(s_bn, bn_steps(i) + 2)
                nc.scalar.activation(rstd[(i - 1) % XS][0:rows, 0:r], mv[i % 2][0:rows, 0:r, 1], ACT.Sqrt,
                                     bias=eps_sb[0:rows, :]).then_inc(s_std, 1)

            act.wait_ge(s_eps, 1)
            std_chunk(0)
            for i in range(NCHUNK + 1):
                if i < NCHUNK:
                    std_chunk(i + 1)
                    act.wait_ge(s_bn, bn_steps(i + 1) + 4)
                else:
                    act.wait_ge(s_bn, bn_steps(i) + 6)
                if i == 0:
                    relu_chunk(xr[:, :].rearrange("p (r d) -> p r d", r=1), REST_N, 1, XS - 1, 1)
                    act.dma_start(h_table[ROWS * P:N, :], xr[:, :]).then_inc(s_hr, 16)
                else:
                    slot = (i - 1) % XS
                    relu_chunk(xc[slot], P, CR, slot, i + 1)
                    act.dma_start(h_rows[:, (i - 1) * CR:i * CR, :], xc[slot][:, :, :]).then_inc(s_hd[slot], 16)

            act.wait_ge(s_flag, 1)
            windows = act.value_load(flag_i[0:1, 0:1], min_val=0, max_val=1)

            def stage(s, j0, j1):
                c0, n = j0 * GT, (j1 - j0) * GT
                nc.scalar.copy(src_now[:, c0:c0 + n], srcT[:, bass.ds(s * ST + c0, n)]).then_inc(s_stage, 1)

            def superstep(s, groups, after):
                work = not (isinstance(s, int) and s == 0) and groups == SG
                if work:
                    act_copy_h(act, 0, s - 1, P)
                if groups == SG:
                    hold(act, s_agg, s * SG + GT)
                    stage(s + 1, 0, min(GT, after))
                if work:
                    act_gelu(act, 0, s - 1, P)
                    act_affine(act, 0, s - 1, P)
                    act_copy_h(act, 1, s - 1, P)
                    act_gelu(act, 1, s - 1, P)
                    act_affine(act, 1, s - 1, P)
                if groups == SG and after > GT:
                    hold(act, s_agg, s * SG + SG)
                    stage(s + 1, GT, after)

            def finish(q, k, rows):
                act_copy_h(act, q, k, rows)
                act_gelu(act, q, k, rows)
                act_affine(act, q, k, rows)

            with act.If(windows):
                stage(0, 0, GT)
                stage(0, GT, SG)
                superstep(0, SG, SG)
                with act.Fori(1, S_LAST - 1) as s:
                    superstep(s, SG, SG)
                superstep(S_LAST - 1, SG, LAST_G)
                act_copy_h(act, 0, S_LAST - 1, P)
                act_copy_h(act, 1, S_LAST - 1, P)
                for q in range(2):
                    act_gelu(act, q, S_LAST - 1, P)
                    act_affine(act, q, S_LAST - 1, P)
                finish(0, NPAIR, REST_N)
            with act.Else():
                nc.scalar.copy(g_src, srcT[:, 0:1]).then_inc(g_staged, 1)
                with act.Fori(0, NT) as k:
                    act.wait_ge(g_mm, k + 1)
                    for i in range(2):
                        last = nc.scalar.copy(g_sums[:, i * 512:(i + 1) * 512], p_wide[:, i * 512:(i + 1) * 512])
                    last.then_inc(g_copied, 1)
                    nc.scalar.copy(g_src, srcT[:, bass.ds(k + 1, 1)]).then_inc(g_staged, 1)

                def node_tile(q, k, n, rows):
                    act_copy_h(act, q, k, rows)
                    act.wait_ge(g_aT, n + 1)
                    nc.scalar.copy(aggT_nt[q].rearrange("p (c r) -> p c r", c=KB)[:, :, 0:rows],
                                   p_wide[:, :].rearrange("p (c r) -> p c r", c=KB)[:, :, 0:rows]).then_inc(g_aTc, 1)
                    act_gelu(act, q, k, rows)
                    act_affine(act, q, k, rows)

                with act.Fori(0, NPAIR) as i:
                    for q in range(2):
                        node_tile(q, i, i * 2 + q, P)
                node_tile(0, NPAIR, 2 * NPAIR, REST_N)


        def dve_sum(dve, q, k, rows):
            hold(dve, s_ld[q], k * 32 + 32)
            dve.wait_ge(s_mm[q], k + 1)
            nc.vector.tensor_tensor(z_nt[q][0:rows, :], p_out[q][0:rows, 0:D], h_nt[q][0:rows, :],
                                    ALU.add).then_inc(s_z[q], 1)
            dve.wait_ge(s_z[q], k * 2 + 1)
            nc.vector.tensor_tensor(z_nt[q][0:rows, :], z_nt[q][0:rows, :], bias_sb[0:rows, :],
                                    ALU.add).then_inc(s_z[q], 1)

        def dve_norm(dve, q, k, rows):
            dve.wait_ge(s_gelu[q], k + 1)
            nc.vector.bn_stats(bn_nt[q][0:rows, :], z_nt[q][0:rows, :]).then_inc(s_nrm[q], 1)
            hold(dve, s_nrm[q], k * 5 + 1)
            nc.vector.bn_aggr(mv_nt[q][0:rows, :], bn_nt[q][0:rows, :]).then_inc(s_nrm[q], 1)
            dve.wait_ge(s_nrm[q], k * 5 + 3)
            nc.vector.reciprocal(rstd_nt[q][0:rows, :], rstd_nt[q][0:rows, :]).then_inc(s_nrm[q], 1)
            dve.wait_ge(s_nrm[q], k * 5 + 4)
            nc.vector.scalar_tensor_tensor(out=nmr_nt[q][0:rows, :], in0=mv_nt[q][0:rows, 0:1], scalar=-1.0,
                                           in1=rstd_nt[q][0:rows, :], op0=ALU.mult, op1=ALU.mult
                                           ).then_inc(s_nrm[q], 1)

        def dve_result(dve, q, k, rows):
            y = y_nt[q][0:rows, :]
            dve.wait_ge(s_aff[q], k * 3 + 1)
            nc.vector.tensor_tensor(y, y, gamma_sb[0:rows, :], ALU.mult).then_inc(s_aff[q], 1)
            dve.wait_ge(s_aff[q], k * 3 + 2)
            nc.vector.tensor_tensor(y, y, beta_sb[0:rows, :], ALU.add).then_inc(s_aff[q], 1)
            dve.wait_ge(s_aff[q], k * 3 + 3)
            nc.vector.tensor_tensor(y, y, x_nt[q][0:rows, :], ALU.add).then_inc(s_res[q], 1)

        @block.vector
        def _(dve):
            def stats_chunk(i, buf, rows, r):
                if i:
                    dve.wait_ge(s_bn, bn_steps(i))
                for n in range(r):
                    last = nc.vector.bn_stats(bn[0:rows, n, :], buf[0:rows, n, :])
                last.then_inc(s_bn, 1)
                dve.wait_ge(s_bn, bn_steps(i) + 1)
                for n in range(r):
                    last = nc.vector.bn_aggr(mv[i % 2][0:rows, n, :], bn[0:rows, n, :])
                last.then_inc(s_bn, 1)

            def scale_chunk(i, done):
                rows, r = (REST_N, 1) if i == 0 else (P, CR)
                inv = rstd[(i - 1) % XS][0:rows, 0:r]
                dve.wait_ge(s_std, i + 1)
                nc.vector.reciprocal(inv, inv).then_inc(s_bn, 1)
                dve.wait_ge(s_bn, done + 1)
                nc.vector.scalar_tensor_tensor(out=nmr[(i - 1) % XS][0:rows, 0:r], in0=mv[i % 2][0:rows, 0:r, 0],
                                               scalar=-1.0, in1=inv, op0=ALU.mult, op1=ALU.mult
                                               ).then_inc(s_bn, 1)

            def copy_list(n):
                for i, (m, b0, nb) in enumerate(tr_batches):
                    if m == n:
                        dve.wait_ge(s_tr, i + 1)
                        nc.vector.tensor_copy(listT[n][:, b0 * P:(b0 + nb) * P],
                                              tr_bank(i)[:, 0:nb * P]).then_inc(s_trc, 1)

            dve.memset(acc[:, :, :], 0.0).then_inc(s_shift, 3)
            dve.wait_ge(s_xr, 16)
            stats_chunk(0, xr[:, :].rearrange("p (r d) -> p r d", r=1), REST_N, 1)
            for c in range(NCHUNK):
                dve.wait_ge(s_x[c % XS], 16 * (c // XS + 1))
                stats_chunk(c + 1, xc[c % XS], P, CR)
                scale_chunk(c, bn_steps(c + 1) + 2)
                if c == 1:
                    copy_list(0)
                if c == 3:
                    copy_list(1)
            scale_chunk(NCHUNK, bn_steps(NCHUNK) + 4)
            dve.wait_ge(s_const, 7)
            dve.wait_ge(s_trc, 2 * NBATCH)
            dve.wait_ge(s_first, 1)
            nc.vector.tensor_tensor(dloc[:, :, :], dstT[:, 0:NT].rearrange("p (g t) -> p g t", t=GT),
                                    p_first[:, 0:NG].unsqueeze(2).to_broadcast([P, NG, GT]), ALU.subtract)
            nc.vector.tensor_tensor(offs[:, :], p_first[:, 0:NG], step_base[:, 0:NG], ALU.add).then_inc(s_chk, 1)
            dve.wait_ge(s_chk, 1)
            nc.vector.tensor_tensor(room[:, :], offs[:, :],
                                    least[:, :, :].rearrange("p s j -> p (s j)")[:, 0:NG],
                                    ALU.subtract).then_inc(s_chk, 1)
            nc.vector.tensor_copy(offs_i[:, :], offs[0:1, :])
            dve.wait_ge(s_chk, 2)
            flat = dloc[:, :, :].rearrange("p g t -> p (g t)")
            nc.vector.tensor_reduce(lim[:, 0:1], flat, AX, ALU.min)
            nc.vector.tensor_reduce(lim[:, 1:2], flat, AX, ALU.max)
            nc.vector.tensor_reduce(lim[:, 2:3], room[:, :], AX, ALU.min)
            nc.vector.tensor_reduce(lim[:, 3:4], offs[:, :], AX, ALU.max).then_inc(s_chk, 1)
            dve.wait_ge(s_chk, 3)
            nc.vector.tensor_scalar(okay[:, 0:1], lim[:, 0:1], 0.0, None, ALU.is_ge)
            nc.vector.tensor_scalar(okay[:, 1:2], lim[:, 1:2], float(WIN - 1), None, ALU.is_le)
            nc.vector.tensor_scalar(okay[:, 2:3], lim[:, 2:3], 0.0, None, ALU.is_ge)
            nc.vector.tensor_scalar(okay[:, 3:4], lim[:, 3:4], float(AW - WIN), None, ALU.is_le).then_inc(s_chk, 1)
            for n in range(3):
                dve.wait_ge(s_chk, 4 + n)
                nc.vector.tensor_tensor(okay[:, 0:1], okay[:, 0:1], okay[:, n + 1:n + 2], ALU.mult).then_inc(s_chk, 1)
            dve.wait_ge(s_chk, 7)
            nc.vector.memset(lim[:, :], 0.0).then_inc(s_chk, 1)
            dve.wait_ge(s_cnt, 1)
            nc.vector.tensor_scalar(flag_i[:, :], p_out[0][0:1, 0:1], float(P), None, ALU.is_ge).then_inc(s_flag, 1)
            copy_list(2)
            dve.wait_ge(s_trc, 3 * NBATCH)
            dve.wait_ge(s_par, 16 * 6)
            dve.wait_ge(s_flag, 1)
            windows = dve.value_load(flag_i[0:1, 0:1], min_val=0, max_val=1)
            comp_b = comp_sb[:, :, :].rearrange("p r b -> p b r")

            def coefficients(s, tiles):
                if not (isinstance(s, int) and s == 0):
                    dve.wait_ge(s_M, s * SG)
                nc.vector.tensor_tensor(typ_is[:, 0:tiles, :],
                                        typT[:, bass.ds(s * ST, tiles)].unsqueeze(2).to_broadcast([P, tiles, NR]),
                                        iota_rel[:, :].unsqueeze(1).to_broadcast([P, tiles, NR]),
                                        ALU.is_equal).then_inc(s_coef, 1)
                dve.wait_ge(s_coef, s * 3 + 1)
                for b in range(NB):
                    last = nc.vector.tensor_tensor(typ_comp[:, 0:tiles, b, :], typ_is[:, 0:tiles, :],
                                                   comp_b[:, b:b + 1, :].to_broadcast([P, tiles, NR]), ALU.mult)
                last.then_inc(s_coef, 1)
                dve.wait_ge(s_coef, s * 3 + 2)
                nc.vector.tensor_reduce(coef[:, 0:tiles, :].rearrange("p t b -> p (t b)"),
                                        typ_comp[:, 0:tiles, :, :].rearrange("p t b r -> p (t b) r"),
                                        AX, ALU.add).then_inc(s_coef, 1)

            def make_M(s, j):
                g = s * SG + j
                if not (isinstance(s, int) and s == 0 and j == 0):
                    dve.wait_ge(s_M, g)
                nc.vector.tensor_tensor(here[:, :, :],
                                        dloc[:, bass.ds(g, 1), :].rearrange("p a t -> p (a t)")
                                        .unsqueeze(2).to_broadcast([P, GT, WIN]),
                                        iota_win[:, :].unsqueeze(1).to_broadcast([P, GT, WIN]),
                                        ALU.is_equal).then_inc(s_here, 1)
                if j == 0:
                    hold(dve, s_coef, s * 3 + 3)
                if not (isinstance(s, int) and s == 0 and j < MS):
                    hold(dve, s_agg, g - 1 if j < 2 else g - 2)
                dve.wait_ge(s_here, g + 1)
                for b in range(NB):
                    last = nc.vector.tensor_tensor(M[:, j % MS, :, b, :], here[:, :, :],
                                                   coef[:, j * GT:(j + 1) * GT, b].unsqueeze(2)
                                                   .to_broadcast([P, GT, WIN]), ALU.mult)
                last.then_inc(s_M, 1)

            def flush(s, j, off):
                g = s * SG + j
                if j == 0:
                    hold(dve, s_shift, s * 3 + 3)
                if not (isinstance(s, int) and s == 0 and j == 0):
                    hold(dve, s_flush, g)
                dve.wait_ge(s_agg, g + 1)
                window = acc[:, :, bass.ds(off, WIN)]
                nc.vector.tensor_tensor(window, window,
                                        p_sum[j % MS][:, 0:KB * WIN].rearrange("p (c w) -> p c w", c=KB),
                                        ALU.add).then_inc(s_flush, 1)

            def superstep(s, groups):
                first = isinstance(s, int) and s == 0
                coefficients(s, groups * GT)
                _, off = nc.values_load_multi_w_load_instructions(
                    offs_i[0:1, bass.ds(s * SG, groups)], engines=[mybir.EngineType.DVE],
                    min_val=0, max_val=AW - WIN)
                make_M(s, 0)
                for j in range(groups):
                    if j + 1 < groups:
                        make_M(s, j + 1)
                    flush(s, j, off[j])
                    if first or groups < SG:
                        continue
                    for q, at in ((0, SETTLED + 2), (1, SETTLED + 5)):
                        if j == at:
                            dve_sum(dve, q, s - 1, P)
                        if j == at + 1:
                            dve_norm(dve, q, s - 1, P)
                            dve_result(dve, q, s - 1, P)
                if groups < SG:
                    return
                if not first:
                    hold(dve, s_mm[0], s)
                    hold(dve, s_mm[1], s)
                dve.wait_ge(s_flush, s * SG + SG)
                nc.vector.tensor_copy(acc[:, :, 0:STEP], acc[:, :, STEP:2 * STEP]).then_inc(s_shift, 1)
                dve.wait_ge(s_shift, s * 3 + 4)
                nc.vector.tensor_copy(acc[:, :, STEP:AW - STEP], acc[:, :, 2 * STEP:AW]).then_inc(s_shift, 1)
                dve.wait_ge(s_shift, s * 3 + 5)
                nc.vector.memset(acc[:, :, AW - STEP:AW], 0.0).then_inc(s_shift, 1)

            with dve.If(windows):
                superstep(0, SG)
                with dve.Fori(1, S_LAST) as s:
                    superstep(s, SG)
                superstep(S_LAST, LAST_G)
                for q, k, rows in ((0, S_LAST - 1, P), (1, S_LAST - 1, P), (0, NPAIR, REST_N)):
                    dve_sum(dve, q, k, rows)
                    dve_norm(dve, q, k, rows)
                    dve_result(dve, q, k, rows)
            with dve.Else():
                nc.vector.memset(g_zero, 0.0).then_inc(g_zeroed, 1)
                with dve.Fori(0, NT) as k:
                    nc.vector.tensor_copy(g_dst[:, :], dstT[:, bass.ds(k, 1)])
                    nc.vector.tensor_copy(g_wide, dstT[:, bass.ds(k, 1)].to_broadcast([P, P])).then_inc(g_wid, 1)
                    nc.vector.tensor_tensor(g_ti, typT[:, bass.ds(k, 1)].to_broadcast([P, NR]), iota_rel[:, :],
                                            ALU.is_equal).then_inc(g_mk, 1)
                    dve.wait_ge(g_mk, k * 9 + 1)
                    nc.vector.tensor_tensor(g_tc, g_ti.unsqueeze(1).to_broadcast([P, NB, NR]), comp_b,
                                            ALU.mult).then_inc(g_mk, 1)
                    dve.wait_ge(g_mk, k * 9 + 2)
                    nc.vector.tensor_reduce(g_coef[:, :], g_tc, AX, ALU.add).then_inc(g_mk, 1)
                    hold(dve, g_mk, k * 9 + 3)
                    dve.wait_ge(g_tr, k + 1)
                    nc.vector.tensor_scalar(g_same, p_sum[0][:, 0:P], g_dst[:, 0:1], None,
                                            ALU.is_equal).then_inc(g_mk, 1)
                    dve.wait_ge(g_mk, k * 9 + 4)
                    nc.vector.tensor_tensor(g_prev, g_same, below[:, :], ALU.mult).then_inc(g_mk, 1)
                    dve.wait_ge(g_mk, k * 9 + 5)
                    nc.vector.tensor_reduce(g_first[:, 0:1], g_prev, AX, ALU.max)
                    nc.vector.tensor_tensor(g_first[:, 1:2], waste[:, :], g_dst[:, :], ALU.subtract).then_inc(g_mk, 1)
                    dve.wait_ge(g_mk, k * 9 + 6)
                    nc.vector.tensor_tensor(g_first[:, 0:1], g_first[:, 0:1], g_first[:, 1:2], ALU.mult).then_inc(g_mk, 1)
                    dve.wait_ge(g_mk, k * 9 + 7)
                    nc.vector.tensor_tensor(g_dst_i, g_first[:, 0:1], g_dst[:, :], ALU.add).then_inc(g_mk, 1)
                    for b in range(NB):
                        last = nc.vector.tensor_scalar(g_M[:, b, :], g_same, g_coef[:, b:b + 1], None, ALU.mult)
                    last.then_inc(g_mk, 1)
                    hold(dve, g_added, k * 16 + 16)

                def node_tile(q, k, rows):
                    dve_sum(dve, q, k, rows)
                    dve_norm(dve, q, k, rows)
                    dve_result(dve, q, k, rows)

                with dve.Fori(0, NPAIR) as i:
                    for q in range(2):
                        node_tile(q, i, P)
                node_tile(0, NPAIR, REST_N)


_INS = ["x", "src", "dst", "edge_type_8", "L0_gnn_basis", "L0_gnn_comp", "L0_gnn_loop_w", "L0_gnn_h_bias",
        "L0_gnn_ln_gamma", "L0_gnn_ln_beta"]


def kernel(**inputs):
    import numpy as _np
    import concourse.bacc as _bacc
    from concourse import mybir as _mybir
    from concourse.bass_utils import run_bass_kernel_spmd as _run

    nc = _bacc.Bacc("TRN2", target_bir_lowering=False, num_devices=1)
    arrays, args = {}, []
    for name in _INS:
        a = _np.ascontiguousarray(inputs[name])
        arrays[f"in_{name}"] = a
        args.append(nc.dram_tensor(f"in_{name}", a.shape, _mybir.dt.from_np(a.dtype), kind="ExternalInput").ap())
    shape = inputs["x"].shape
    args.append(nc.dram_tensor("out_0", shape, _mybir.dt.from_np(_np.dtype("float32")), kind="ExternalOutput").ap())
    build_rgcn(nc, *args)
    r = _run(nc, [arrays], core_ids=[0])
    return r.results[0]["out_0"]
```

```python
from contextlib import ExitStack

import numpy as np

import concourse.bass as bass
from concourse import mybir

F32 = mybir.dt.float32
I32 = mybir.dt.int32
ALU = mybir.AluOpType
ACT = mybir.ActivationFunctionType
AX = mybir.AxisListType.X

P = 128
EPS = 1e-5


def build_rgcn(nc, x, src, dst, etype, basis, comp, loop_w, h_bias, ln_gamma, ln_beta, out):
    N, D = x.shape
    E = src.shape[0]
    NB = basis.shape[0]
    NR = comp.shape[0]
    HALVES = D // P
    KB = HALVES * NB

    GT = 6
    SG = 11
    WIN = 32
    STEP = 2 * P
    ST = SG * GT
    NG = -(-E // (GT * P))
    NT = NG * GT
    S_LAST = N // STEP
    LAST_G = NG - S_LAST * SG
    LAST_T = -(-E // P) - (NG - 1) * GT
    assert 0 < LAST_G <= SG and ST <= P
    AW = 2 * STEP + 2 * WIN
    SETTLED = 4
    SETTLED_LAST = 2
    assert SETTLED_LAST + 3 <= LAST_G
    EB = -(-NT // P)
    FULL_T, REST_E = E // P, E % P
    MAIN_T = (FULL_T // P) * P
    REST_T = FULL_T - MAIN_T

    ROWS = N // P
    REST_N = N - ROWS * P
    CR = 6
    NCHUNK = ROWS // CR
    XS = 6
    assert ROWS % CR == 0 and NCHUNK > XS
    NPAIR = N // STEP
    assert N - NPAIR * STEP == REST_N
    AGG_ROWS = -(-(N + P) // P) * P
    DB = NB * D

    h_table = nc.dram_tensor("h_table", [N, D], F32, kind="Internal").ap()
    agg_table = nc.dram_tensor("agg_table", [AGG_ROWS, DB], F32, kind="Internal").ap()

    ctx = ExitStack()
    with ctx:
        def sb(name, shape, dt=F32):
            return ctx.enter_context(nc.sbuf_tensor(name, shape, dt))

        def ps(name, shape):
            return ctx.enter_context(nc.psum_tensor(name, shape, F32))

        def sem(name):
            return ctx.enter_context(nc.semaphore(name))

        ident = sb("ident", [P, P])
        ones = sb("ones", [P, P])
        below = sb("below", [P, P])
        iota_i = sb("iota_i", [P, (S_LAST + 1) * SG], I32)
        iota_win = sb("iota_win", [P, WIN])
        iota_rel = sb("iota_rel", [P, NR])
        waste_i = sb("waste_i", [P, 1], I32)
        waste = sb("waste", [P, 1])
        step_base = sb("step_base", [P, (S_LAST + 1) * SG])
        least = sb("least", [P, S_LAST + 1, SG])
        basis_sb = sb("basis_sb", [P, NB, HALVES, D])
        loop_sb = sb("loop_sb", [P, HALVES, D])
        comp_sb = sb("comp_sb", [P, NR, NB])
        bias_sb = sb("bias_sb", [P, D])
        gamma_sb = sb("gamma_sb", [P, D])
        beta_sb = sb("beta_sb", [P, D])

        acc = sb("acc", [P, KB, AW])
        typ_comp_mem = sb("typ_comp", [P, ST * NB * NR])
        acc_mem = acc[:, :, :].rearrange("p c n -> p (c n)")
        assert 2 * EB * P <= KB * AW
        rawf = [m.rearrange("p (b e) -> p b e", e=P) for m in (
            acc_mem[:, 0:EB * P], acc_mem[:, EB * P:2 * EB * P], typ_comp_mem[:, 0:EB * P])]
        raw = [m.bitcast(I32) for m in rawf]
        srcT = sb("srcT", [P, EB * P])
        dstT = sb("dstT", [P, EB * P])
        typT = sb("typT", [P, EB * P])
        dloc = sb("dloc", [P, NG, GT])
        room = sb("room", [P, NG])
        offs = sb("offs", [P, NG])
        offs_i = sb("offs_i", [1, NG], I32)
        lim = sb("lim", [P, 4])
        okay = sb("okay", [P, 4])
        flag_i = sb("flag_i", [1, 1], I32)

        xc = [sb(f"xc{i}", [P, CR, D]) for i in range(XS)]
        xr = sb("xr", [REST_N, D])
        bn = sb("bn", [P, CR, 6])
        mv = [sb(f"mv{i}", [P, CR, 2]) for i in range(2)]
        eps_sb = sb("eps_sb", [P, 1])
        rstd = [sb(f"rstd{i}", [P, CR]) for i in range(XS)]
        nmr = [sb(f"nmr{i}", [P, CR]) for i in range(XS)]

        bn_g = sb("bn_g", [P, GT, 6])
        mv_g = [sb(f"mv_g{i}", [P, GT, 2]) for i in range(2)]
        RS = 3
        rstd_g = [sb(f"rstd_g{i}", [P, GT]) for i in range(RS)]
        nmr_g = [sb(f"nmr_g{i}", [P, GT]) for i in range(RS)]

        src_now = sb("src_now", [P, ST], I32)
        gath = sb("gath", [P, SG, GT, D])
        typ_is = sb("typ_is", [P, ST, NR])
        typ_comp = typ_comp_mem[:, :].rearrange("p (t b r) -> p t b r", b=NB, r=NR)
        coef = sb("coef", [P, ST, NB])
        here = sb("here", [P, GT, WIN])
        MS = 3
        M = sb("M", [P, MS, GT, NB, WIN])

        SLOTS = range(3)
        REST = 2
        PAIR = ((0, P), (1, P))
        x_nt = [sb(f"x_nt{q}", [P, D]) for q in SLOTS]
        h_nt = [sb(f"h_nt{q}", [P, D]) for q in SLOTS]
        hT_nt = [sb(f"hT_nt{q}", [P, HALVES, P]) for q in SLOTS]
        z_nt = [sb(f"z_nt{q}", [P, D]) for q in SLOTS]
        bn_nt = [sb(f"bn_nt{q}", [P, 6]) for q in SLOTS]
        mv_nt = [sb(f"mv_nt{q}", [P, 2]) for q in SLOTS]
        rstd_nt = [sb(f"rstd_nt{q}", [P, 1]) for q in SLOTS]
        nmr_nt = [sb(f"nmr_nt{q}", [P, 1]) for q in SLOTS]
        y_nt = [sb(f"y_nt{q}", [P, D]) for q in SLOTS]

        g_src = src_now[:, 0:1]
        g_dst_i = src_now[:, 1:2]
        g_dst = sb("g_dst", [P, 1])
        g_first = sb("g_first", [P, 2])
        g_coef = sb("g_coef", [P, NB])
        g_tc = typ_comp[:, 0, :, :]
        g_ti = typ_is[:, 0, :]
        g_rows = gath[:, 0, 0, :]
        g_wide = gath[:, 1, 0, 0:P]
        g_same = gath[:, 1, 1, 0:P]
        g_prev = gath[:, 1, 2, 0:P]
        g_M = gath[:, 2, 0:2, :].rearrange("p t (a e) -> p (t a) e", a=2)
        g_sums = gath[:, 3, 0:NB, :].rearrange("p t d -> p (t d)")
        g_zero = gath[:, 4, 0:NB, :].rearrange("p t d -> p (t d)")
        agg_nt = [gath[:, 5 + q, 0:NB, :].rearrange("p t d -> p (t d)") for q in SLOTS]
        aggT_nt = [gath[:, 8 + q, 0:NB, :].rearrange("p t d -> p (t d)") for q in SLOTS]

        p_sum = [ps(f"p_sum{i}", [P, 512]) for i in range(MS)]
        p_out = [ps(f"p_out{q}", [P, 512]) for q in SLOTS]
        p_wide = ps("p_wide", [P, 1024])

        s_const = sem("s_const")
        s_comp = sem("s_comp")
        s_par = sem("s_par")
        s_src0 = sem("s_src0")
        s_raw = [sem(f"s_raw{n}") for n in range(3)]
        s_pad = sem("s_pad")
        s_flt = sem("s_flt")
        s_tr = sem("s_tr")
        s_trc0 = sem("s_trc0")
        s_trc = sem("s_trc")
        s_x = [sem(f"s_x{i}") for i in range(XS)]
        s_xr = sem("s_xr")
        s_bn = sem("s_bn")
        s_eps = sem("s_eps")
        s_std = sem("s_std")
        s_h = sem("s_h")
        s_hd = [sem(f"s_hd{i}") for i in range(XS)]
        s_hr = sem("s_hr")
        s_first = sem("s_first")
        s_chk = sem("s_chk")
        s_cnt = sem("s_cnt")
        s_flag = sem("s_flag")
        held = sem("held")

        s_stage = sem("s_stage")
        s_gath = [sem(f"s_gath{j}") for j in range(SG)]
        s_bn_g = sem("s_bn_g")
        s_std_g = sem("s_std_g")
        s_rows = sem("s_rows")
        s_coef = sem("s_coef")
        s_here = sem("s_here")
        s_M = sem("s_M")
        s_agg = sem("s_agg")
        s_flush = sem("s_flush")
        s_shift = sem("s_shift")

        s_ld = [sem(f"s_ld{q}") for q in SLOTS]
        s_hT = [sem(f"s_hT{q}") for q in SLOTS]
        s_hTc = [sem(f"s_hTc{q}") for q in SLOTS]
        s_mm = [sem(f"s_mm{q}") for q in SLOTS]
        s_z = [sem(f"s_z{q}") for q in SLOTS]
        s_gelu = [sem(f"s_gelu{q}") for q in SLOTS]
        s_nrm = [sem(f"s_nrm{q}") for q in SLOTS]
        s_aff = [sem(f"s_aff{q}") for q in SLOTS]
        s_res = [sem(f"s_res{q}") for q in SLOTS]
        s_out = [sem(f"s_out{q}") for q in SLOTS]

        g_zeroed = sem("g_zeroed")
        g_clear = sem("g_clear")
        g_staged = sem("g_staged")
        g_gath = sem("g_gath")
        g_wid = sem("g_wid")
        g_tr = sem("g_tr")
        g_mk = sem("g_mk")
        g_mm = sem("g_mm")
        g_copied = sem("g_copied")
        g_added = sem("g_added")
        g_ld = [sem(f"g_ld{q}") for q in SLOTS]
        g_aT = sem("g_aT")
        g_aTc = sem("g_aTc")

        block = ctx.enter_context(nc.Block())

        def hold(eng, semaphore, value):
            eng.wait_ge(semaphore, value)
            eng.sem_inc(held, 1)

        def tiles_in(groups, j):
            return LAST_T if groups < SG and j == groups - 1 else GT

        def first_rows_in(eng):
            for j in range(SG):
                eng.wait_ge(s_gath[j], 16 * GT)

        def bn_steps(i):
            return 0 if i == 0 else 4 * i - 2

        pads = (0, N - 1, NR)

        x_rows = x[0:ROWS * P, :].rearrange("(p r) d -> p r d", p=P)
        h_rows = h_table[0:ROWS * P, :].rearrange("(p r) d -> p r d", p=P)

        SRC, DST, TYP = range(3)
        PARTS = ((SRC, 0, 1), (DST, 0, EB), (SRC, 1, EB), (TYP, 0, EB))
        G_BATCH = 4
        batches = [(part, n, b, min(G_BATCH, b1 - b)) for part, (n, b0, b1) in enumerate(PARTS)
                   for b in range(b0, b1, G_BATCH)]
        ends = [max(i for i, batch in enumerate(batches) if batch[0] == part) for part in range(len(PARTS))]
        listT = (srcT, dstT, typT)

        def tr_bank(i):
            return (p_wide[:, 0:512], p_wide[:, 512:1024], p_sum[0][:, :], p_sum[1][:, :])[i % 4]


        def sp_load_nt(sp, q, row, rows):
            sp.dma_start(x_nt[q][0:rows, :], x[bass.ds(row, rows), :]).then_inc(s_ld[q], 16)
            sp.dma_start(h_nt[q][0:rows, :], h_table[bass.ds(row, rows), :]).then_inc(s_ld[q], 16)

        def sp_store_nt(sp, q, k, row, rows):
            sp.wait_ge(s_res[q], k + 1)
            sp.dma_start(out[bass.ds(row, rows), :], y_nt[q][0:rows, :]).then_inc(s_out[q], 16)

        def sp_node_tiles(sp, k, row, tiles, sums=None):
            for i, (q, rows) in enumerate(tiles):
                if sums is not None:
                    sums(q, row + i * P, rows)
                sp_load_nt(sp, q, row + i * P, rows)
            for i, (q, rows) in enumerate(tiles):
                sp_store_nt(sp, q, k, row + i * P, rows)
            for q, rows in tiles:
                hold(sp, s_out[q], k * 16 + 16)

        @block.sync
        def _(sp):
            def load_list(n, a, b0):
                sp.dma_start(raw[n][:, b0:MAIN_T // P, :],
                             a[b0 * P * P:MAIN_T * P].rearrange("(b t e) -> t b e", t=P, e=P)).then_inc(s_raw[n], 16)
                sp.wait_ge(s_pad, n + 1)
                if REST_T:
                    sp.dma_start(raw[n][0:REST_T, EB - 1, :],
                                 a[MAIN_T * P:FULL_T * P].rearrange("(t e) -> t e", e=P)).then_inc(s_raw[n], 16)
                if REST_E:
                    sp.dma_start(raw[n][REST_T:REST_T + 1, EB - 1, 0:REST_E],
                                 a[FULL_T * P:E].rearrange("(t e) -> t e", t=1)).then_inc(s_raw[n], 16)

            def load_x(c):
                if c >= XS:
                    sp.wait_ge(s_hd[c % XS], 16 * (c // XS))
                sp.dma_start(xc[c % XS][:, :, :], x_rows[:, c * CR:(c + 1) * CR, :]).then_inc(s_x[c % XS], 16)

            sp.dma_start(raw[SRC][:, 0, :], src[0:P * P].rearrange("(t e) -> t e", e=P)).then_inc(s_src0, 16)
            sp.dma_start(xr[:, :], x[ROWS * P:N, :]).then_inc(s_xr, 16)
            load_x(0)
            load_list(DST, dst, 0)
            load_x(1)
            load_x(2)
            load_list(SRC, src, 1)
            load_list(TYP, etype, 0)
            sp.dma_start(comp_sb[:, :, :].rearrange("p r b -> p (r b)"),
                         comp.rearrange("r b -> (r b)").partition_broadcast(P)).then_inc(s_comp, 16)
            for c in range(3, NCHUNK):
                load_x(c)
            for to, what in ((basis_sb[:, :, :, :], basis.rearrange("b (h p) o -> p b h o", p=P)),
                             (loop_sb[:, :, :], loop_w.rearrange("(h p) o -> p h o", p=P)),
                             (bias_sb[:, :], h_bias.partition_broadcast(P)),
                             (gamma_sb[:, :], ln_gamma.partition_broadcast(P)),
                             (beta_sb[:, :], ln_beta.partition_broadcast(P))):
                sp.dma_start(to, what).then_inc(s_par, 16)

            sp.wait_ge(s_flag, 1)
            windows = sp.value_load(flag_i[0:1, 0:1], min_val=0, max_val=1)
            for i in range(XS):
                sp.wait_ge(s_hd[i], 16 * len(range(i, NCHUNK, XS)))
            sp.wait_ge(s_hr, 16)
            with sp.If(windows):
                sp_load_nt(sp, REST, NPAIR * STEP, REST_N)
                with sp.Fori(1, S_LAST) as s:
                    sp_node_tiles(sp, s - 1, s * STEP - STEP, PAIR)
                sp_node_tiles(sp, S_LAST - 1, (S_LAST - 1) * STEP, PAIR)
                sp_store_nt(sp, REST, 0, NPAIR * STEP, REST_N)
            with sp.Else():
                sp.wait_ge(g_zeroed, 1)
                sp.dma_start(agg_table.rearrange("(j p) c -> p j c", p=P),
                             g_zero.unsqueeze(1).to_broadcast([P, AGG_ROWS // P, DB])).then_inc(g_clear, 16)
                sp.wait_ge(g_added, 16 * NT)

                def load_sums(q, row, rows):
                    sp.dma_start(agg_nt[q][0:rows, :], agg_table[bass.ds(row, rows), :]).then_inc(g_ld[q], 16)

                with sp.Fori(0, NPAIR) as i:
                    sp_node_tiles(sp, i, i * STEP, PAIR, load_sums)
                sp_node_tiles(sp, 0, NPAIR * STEP, ((REST, REST_N),), load_sums)
            sp.wait_ge(s_out[0], 16 * NPAIR)
            sp.wait_ge(s_out[1], 16 * NPAIR)
            sp.wait_ge(s_out[REST], 16)


        @block.gpsimd
        def _(pool):
            pool.memset(ident[:, :], 0.0).then_inc(s_const, 1)
            pool.memset(ones[:, :], 1.0).then_inc(s_const, 1)
            pool.wait_ge(s_const, 2)
            pool.affine_select(out=ident[:, :], in_=ident[:, :], compare_op=ALU.not_equal, fill=1.0,
                               base=0, pattern=[[-1, P]], channel_multiplier=1).then_inc(s_const, 1)
            pool.memset(eps_sb[:, :], EPS).then_inc(s_eps, 1)
            for n in (DST, SRC, TYP):
                pool.memset(raw[n][:, EB - 1, :], pads[n]).then_inc(s_pad, 1)
            pool.affine_select(out=below[:, :], in_=ones[:, :], compare_op=ALU.is_gt, fill=0.0,
                               base=0, pattern=[[-1, P]], channel_multiplier=1)
            pool.iota(iota_i[:, 0:WIN], pattern=[[1, WIN]], base=0, channel_multiplier=0)
            pool.iota(waste_i[:, :], pattern=[[0, 1]], base=N, channel_multiplier=1).then_inc(s_const, 1)
            pool.wait_ge(s_const, 4)
            pool.tensor_copy(iota_win[:, :], iota_i[:, 0:WIN])
            pool.tensor_copy(iota_rel[:, :], iota_i[:, 0:NR])
            pool.tensor_copy(waste[:, :], waste_i[:, :]).then_inc(s_const, 1)
            pool.wait_ge(s_const, 5)
            pool.iota(iota_i[:, :], pattern=[[-STEP, S_LAST + 1], [0, SG]], base=STEP, channel_multiplier=0)
            pool.memset(least[:, :, :], 0.0).then_inc(s_const, 1)
            pool.wait_ge(s_const, 6)
            pool.tensor_copy(step_base[:, :], iota_i[:, :])
            pool.memset(least[:, S_LAST, SETTLED_LAST:SG], float(STEP))
            pool.memset(least[:, 0:S_LAST, SETTLED:SG], float(STEP)).then_inc(s_const, 1)

            def gather(table, to, index, semaphore):
                pool.indirect_dma_start(to, None, table,
                                        bass.IndirectOffsetOnAxis(ap=index, axis=0)).then_inc(semaphore, 16)

            pool.wait_ge(s_stage, 2)
            for j in range(SG):
                for t in range(GT):
                    gather(x, gath[:, j, t, :], src_now[:, j * GT + t:j * GT + t + 1], s_gath[j])

            pool.wait_ge(s_flag, 1)
            windows = pool.value_load(flag_i[0:1, 0:1], min_val=0, max_val=1)
            for i in range(XS):
                pool.wait_ge(s_hd[i], 16 * len(range(i, NCHUNK, XS)))
            pool.wait_ge(s_hr, 16)

            def superstep(s, groups):
                for j in range(groups):
                    hold(pool, s_agg, (s - 1) * SG + j + 1)
                    if j == 0 or j == GT:
                        hold(pool, s_stage, s * 2 + (1 if j == 0 else 2))
                    for t in range(tiles_in(groups, j)):
                        gather(h_table, gath[:, j, t, :], src_now[:, j * GT + t:j * GT + t + 1], s_gath[j])

            with pool.If(windows):
                with pool.Fori(1, S_LAST) as s:
                    superstep(s, SG)
                superstep(S_LAST, LAST_G)
            with pool.Else():
                first_rows_in(pool)
                pool.wait_ge(g_clear, 16)
                with pool.Fori(0, NT) as k:
                    hold(pool, g_staged, k + 1)
                    gather(h_table, g_rows, g_src, g_gath)
                    hold(pool, g_copied, k + 1)
                    pool.indirect_dma_start(
                        agg_table, bass.IndirectOffsetOnAxis(ap=g_dst_i, axis=0), g_sums, None,
                        compute_op=ALU.add).then_inc(g_added, 16)


        def pe_transpose_h(pe, q, k, rows):
            hold(pe, s_ld[q], (k + 1) * 32)
            for half in range(HALVES):
                last = nc.tensor.transpose(p_out[q][:, D + half * P:D + half * P + rows],
                                           h_nt[q][0:rows, half * P:(half + 1) * P], ident[0:rows, 0:rows])
            last.then_inc(s_hT[q], 1)

        def pe_node_tile_h(pe, q, k, rows):
            hold(pe, s_hTc[q], k + 1)
            for half in range(HALVES):
                nc.tensor.matmul(p_out[q][0:rows, 0:D], hT_nt[q][:, half, 0:rows], loop_sb[:, half, :],
                                 start=(half == 0), stop=False)

        def pe_node_tile_sums(pe, q, rows, sums):
            for half in range(HALVES):
                for b in range(NB):
                    last = nc.tensor.matmul(p_out[q][0:rows, 0:D], sums(half, b), basis_sb[:, b, half, :],
                                            start=False, stop=(half == HALVES - 1 and b == NB - 1))
            last.then_inc(s_mm[q], 1)

        @block.tensor
        def _(pe):
            pe.wait_ge(s_const, 3)
            for i, (part, n, b0, nb) in enumerate(batches):
                pe.wait_ge(s_flt, part + 1)
                if i == 4:
                    pe.wait_ge(s_trc0, 1)
                if i > 4:
                    pe.wait_ge(s_trc, i - 4)
                for b in range(nb):
                    last = nc.tensor.transpose(tr_bank(i)[:, b * P:(b + 1) * P], rawf[n][:, b0 + b, :], ident[:, :])
                last.then_inc(s_tr, 1)
                if i == ends[1] + 1:
                    pe.wait_ge(s_trc, ends[1])
                    nc.tensor.matmul(p_out[REST][:, 0:NG], ones[0:1, :],
                                     dstT[0:1, 0:NT].rearrange("p (g t) -> p g t", t=GT)[:, :, 0],
                                     start=True, stop=True).then_inc(s_first, 1)
                if i == ends[2]:
                    pe.wait_ge(s_chk, 8)
                    nc.tensor.matmul(p_out[0][0:1, 0:1], okay[:, 0:1], ones[:, 0:1], start=True, stop=True).then_inc(s_cnt, 1)

            pe.wait_ge(s_flag, 1)
            windows = pe.value_load(flag_i[0:1, 0:1], min_val=0, max_val=1)
            pe.wait_ge(s_par, 16 * 5)

            def acc_tile(at, rows):
                return lambda half, b: acc[:, half * NB + b, at:at + rows]

            def group(s, j, tiles):
                g = s * SG + j
                if isinstance(s, int) and s == 0:
                    pe.wait_ge(s_rows, j + 1)
                else:
                    hold(pe, s_gath[j], s * (16 * GT) + 16 * tiles)
                free = g - 1 if j < 2 else g - 2
                if not (isinstance(s, int) and s == 0 and j < MS):
                    hold(pe, s_flush, free)
                pe.wait_ge(s_M, g + 1)
                for half in range(HALVES):
                    for t in range(tiles):
                        last = nc.tensor.matmul(p_sum[j % MS][:, half * P:(half + 1) * P],
                                                gath[:, j, t, half * P:(half + 1) * P],
                                                M[:, j % MS, t, :, :].rearrange("p b w -> p (b w)"),
                                                start=(t == 0), stop=(t == tiles - 1))
                last.then_inc(s_agg, 1)

            def superstep(s, groups):
                first = isinstance(s, int) and s == 0
                settled, apart = (SETTLED, 3) if groups == SG else (SETTLED_LAST, 1)
                for j in range(groups):
                    group(s, j, tiles_in(groups, j))
                    for q in range(0 if first else 2):
                        if j == settled + q * apart - 1:
                            pe_transpose_h(pe, q, s - 1, P)
                        if j == settled + q * apart:
                            pe_node_tile_h(pe, q, s - 1, P)
                            hold(pe, s_flush, s * SG + settled)
                            pe_node_tile_sums(pe, q, P, acc_tile(q * P, P))
                    if groups < SG and j == groups - 2:
                        pe_transpose_h(pe, REST, 0, REST_N)
                        pe_node_tile_h(pe, REST, 0, REST_N)

            with pe.If(windows):
                superstep(0, SG)
                with pe.Fori(1, S_LAST) as s:
                    superstep(s, SG)
                superstep(S_LAST, LAST_G)
                pe.wait_ge(s_flush, NG)
                pe_node_tile_sums(pe, REST, REST_N, acc_tile(STEP, REST_N))
            with pe.Else():
                with pe.Fori(0, NT) as k:
                    pe.wait_ge(g_wid, k + 1)
                    nc.tensor.transpose(p_sum[0][:, 0:P], g_wide, ident[:, :]).then_inc(g_tr, 1)
                    hold(pe, g_gath, k * 16 + 16)
                    pe.wait_ge(g_mk, k * 9 + 9)
                    for b in range(NB):
                        last = nc.tensor.matmul(p_wide[:, b * D:(b + 1) * D], g_M[:, b, :], g_rows,
                                                start=True, stop=True)
                    last.then_inc(g_mm, 1)

                def node_tile(q, k, n, rows):
                    pe_transpose_h(pe, q, k, rows)
                    hold(pe, g_ld[q], k * 16 + 16)
                    for c in range(KB):
                        last = nc.tensor.transpose(p_wide[:, c * P:c * P + rows],
                                                   agg_nt[q][0:rows, c * P:(c + 1) * P], ident[0:rows, 0:rows])
                    last.then_inc(g_aT, 1)
                    hold(pe, g_aTc, n + 1)
                    pe_node_tile_h(pe, q, k, rows)
                    pe_node_tile_sums(pe, q, rows, lambda half, b: aggT_nt[q][
                        :, (b * HALVES + half) * P:(b * HALVES + half) * P + rows])

                pe.wait_ge(g_copied, NT)
                with pe.Fori(0, NPAIR) as i:
                    for q in range(2):
                        node_tile(q, i, i * 2 + q, P)
                node_tile(REST, 0, 2 * NPAIR, REST_N)


        def act_copy_h(act, q, k, rows):
            act.wait_ge(s_hT[q], k + 1)
            nc.scalar.copy(hT_nt[q][:, :, 0:rows],
                           p_out[q][:, D:2 * D].rearrange("p (h r) -> p h r", h=HALVES)[:, :, 0:rows]
                           ).then_inc(s_hTc[q], 1)

        def act_gelu(act, q, k, rows):
            act.wait_ge(s_z[q], k * 2 + 2)
            nc.scalar.activation(z_nt[q][0:rows, :], z_nt[q][0:rows, :], ACT.Gelu).then_inc(s_gelu[q], 1)
            act.wait_ge(s_nrm[q], k * 5 + 2)
            nc.scalar.activation(rstd_nt[q][0:rows, :], mv_nt[q][0:rows, 1:2], ACT.Sqrt,
                                 bias=eps_sb[0:rows, :]).then_inc(s_nrm[q], 1)

        def act_affine(act, q, k, rows):
            act.wait_ge(s_nrm[q], k * 5 + 5)
            nc.scalar.activation(y_nt[q][0:rows, :], z_nt[q][0:rows, :], ACT.Identity,
                                 bias=nmr_nt[q][0:rows, :], scale=rstd_nt[q][0:rows, :]).then_inc(s_aff[q], 1)

        @block.scalar
        def _(act):
            def relu_chunk(buf, rows, r, slot, done):
                for i in range(r):
                    last = nc.scalar.activation(buf[0:rows, i, :], buf[0:rows, i, :], ACT.Relu,
                                                bias=nmr[slot][0:rows, i:i + 1], scale=rstd[slot][0:rows, i:i + 1])
                last.then_inc(s_h, 1)
                act.wait_ge(s_h, done)

            def as_float(part):
                n, b0, b1 = PARTS[part]
                if part == 0:
                    act.wait_ge(s_src0, 16)
                else:
                    act.wait_ge(s_raw[n], 16 * (1 + bool(REST_T) + bool(REST_E)))
                nc.scalar.copy(rawf[n][:, b0:b1, :], raw[n][:, b0:b1, :]).then_inc(s_flt, 1)

            def std_chunk(i):
                rows, r = (REST_N, 1) if i == 0 else (P, CR)
                act.wait_ge(s_bn, bn_steps(i) + 2)
                nc.scalar.activation(rstd[(i - 1) % XS][0:rows, 0:r], mv[i % 2][0:rows, 0:r, 1], ACT.Sqrt,
                                     bias=eps_sb[0:rows, :]).then_inc(s_std, 1)

            as_float(0)
            act.wait_ge(s_tr, 1)
            nc.scalar.copy(src_now[:, :], tr_bank(0)[:, 0:ST]).then_inc(s_stage, 2)
            nc.scalar.copy(srcT[:, 0:P], tr_bank(0)[:, 0:P]).then_inc(s_trc0, 1)
            act.wait_ge(s_eps, 1)
            std_chunk(0)
            for i in range(NCHUNK + 1):
                if i < NCHUNK:
                    std_chunk(i + 1)
                    act.wait_ge(s_bn, bn_steps(i + 1) + 4)
                else:
                    act.wait_ge(s_bn, bn_steps(i) + 6)
                if i == 0:
                    relu_chunk(xr[:, :].rearrange("p (r d) -> p r d", r=1), REST_N, 1, XS - 1, 1)
                    act.dma_start(h_table[ROWS * P:N, :], xr[:, :]).then_inc(s_hr, 16)
                else:
                    slot = (i - 1) % XS
                    relu_chunk(xc[slot], P, CR, slot, i + 1)
                    act.dma_start(h_rows[:, (i - 1) * CR:i * CR, :], xc[slot][:, :, :]).then_inc(s_hd[slot], 16)
                if i < 3:
                    as_float(i + 1)

            act.wait_ge(s_flag, 1)
            windows = act.value_load(flag_i[0:1, 0:1], min_val=0, max_val=1)

            def stage(s, j0, j1):
                c0, n = j0 * GT, (j1 - j0) * GT
                nc.scalar.copy(src_now[:, c0:c0 + n], srcT[:, bass.ds(s * ST + c0, n)]).then_inc(s_stage, 1)

            def superstep(s, after):
                act_copy_h(act, 0, s - 1, P)
                hold(act, s_agg, s * SG + GT)
                stage(s + 1, 0, min(GT, after))
                act_gelu(act, 0, s - 1, P)
                act_affine(act, 0, s - 1, P)
                act_copy_h(act, 1, s - 1, P)
                act_gelu(act, 1, s - 1, P)
                act_affine(act, 1, s - 1, P)
                if after > GT:
                    hold(act, s_agg, s * SG + SG)
                    stage(s + 1, GT, after)

            def first_superstep():
                def std_group(j):
                    if j >= RS:
                        act.wait_ge(s_rows, j - RS + 1)
                    act.wait_ge(s_bn_g, bn_steps(j) + 2)
                    nc.scalar.activation(rstd_g[j % RS][:, :], mv_g[j % 2][:, :, 1], ACT.Sqrt,
                                         bias=eps_sb[:, :]).then_inc(s_std_g, 1)

                for j in range(GT):
                    act.wait_ge(s_gath[j], 16 * GT)
                stage(1, 0, GT)
                std_group(0)
                for j in range(SG):
                    if j + 1 < SG:
                        std_group(j + 1)
                        act.wait_ge(s_bn_g, bn_steps(j + 1) + 4)
                    else:
                        act.wait_ge(s_bn_g, bn_steps(j) + 6)
                    for t in range(GT):
                        last = nc.scalar.activation(gath[:, j, t, :], gath[:, j, t, :], ACT.Relu,
                                                    bias=nmr_g[j % RS][:, t:t + 1], scale=rstd_g[j % RS][:, t:t + 1])
                    last.then_inc(s_rows, 1)
                for j in range(GT, SG):
                    act.wait_ge(s_gath[j], 16 * GT)
                stage(1, GT, SG)

            with act.If(windows):
                first_superstep()
                with act.Fori(1, S_LAST - 1) as s:
                    superstep(s, SG)
                superstep(S_LAST - 1, LAST_G)
                act_copy_h(act, 0, S_LAST - 1, P)
                act_copy_h(act, 1, S_LAST - 1, P)
                act_copy_h(act, REST, 0, REST_N)
                for q, k, rows in ((0, S_LAST - 1, P), (1, S_LAST - 1, P), (REST, 0, REST_N)):
                    act_gelu(act, q, k, rows)
                    act_affine(act, q, k, rows)
            with act.Else():
                first_rows_in(act)
                nc.scalar.copy(g_src, srcT[:, 0:1]).then_inc(g_staged, 1)
                with act.Fori(0, NT) as k:
                    act.wait_ge(g_mm, k + 1)
                    for i in range(2):
                        last = nc.scalar.copy(g_sums[:, i * 512:(i + 1) * 512], p_wide[:, i * 512:(i + 1) * 512])
                    last.then_inc(g_copied, 1)
                    nc.scalar.copy(g_src, srcT[:, bass.ds(k + 1, 1)]).then_inc(g_staged, 1)

                def node_tile(q, k, n, rows):
                    act_copy_h(act, q, k, rows)
                    act.wait_ge(g_aT, n + 1)
                    nc.scalar.copy(aggT_nt[q].rearrange("p (c r) -> p c r", c=KB)[:, :, 0:rows],
                                   p_wide[:, :].rearrange("p (c r) -> p c r", c=KB)[:, :, 0:rows]).then_inc(g_aTc, 1)
                    act_gelu(act, q, k, rows)
                    act_affine(act, q, k, rows)

                with act.Fori(0, NPAIR) as i:
                    for q in range(2):
                        node_tile(q, i, i * 2 + q, P)
                node_tile(REST, 0, 2 * NPAIR, REST_N)


        def dve_addends(dve, q, k, rows):
            hold(dve, s_ld[q], k * 32 + 32)
            nc.vector.tensor_tensor(y_nt[q][0:rows, :], h_nt[q][0:rows, :], bias_sb[0:rows, :], ALU.add)
            nc.vector.tensor_tensor(x_nt[q][0:rows, :], x_nt[q][0:rows, :], beta_sb[0:rows, :],
                                    ALU.add).then_inc(s_z[q], 1)

        def dve_sum(dve, q, k, rows):
            hold(dve, s_mm[q], k + 1)
            dve.wait_ge(s_z[q], k * 2 + 1)
            nc.vector.tensor_tensor(z_nt[q][0:rows, :], p_out[q][0:rows, 0:D], y_nt[q][0:rows, :],
                                    ALU.add).then_inc(s_z[q], 1)

        def dve_norm(dve, q, k, rows):
            dve.wait_ge(s_gelu[q], k + 1)
            nc.vector.bn_stats(bn_nt[q][0:rows, :], z_nt[q][0:rows, :]).then_inc(s_nrm[q], 1)
            hold(dve, s_nrm[q], k * 5 + 1)
            nc.vector.bn_aggr(mv_nt[q][0:rows, :], bn_nt[q][0:rows, :]).then_inc(s_nrm[q], 1)
            dve.wait_ge(s_nrm[q], k * 5 + 3)
            nc.vector.reciprocal(rstd_nt[q][0:rows, :], rstd_nt[q][0:rows, :]).then_inc(s_nrm[q], 1)
            dve.wait_ge(s_nrm[q], k * 5 + 4)
            nc.vector.scalar_tensor_tensor(out=nmr_nt[q][0:rows, :], in0=mv_nt[q][0:rows, 0:1], scalar=-1.0,
                                           in1=rstd_nt[q][0:rows, :], op0=ALU.mult, op1=ALU.mult
                                           ).then_inc(s_nrm[q], 1)

        def dve_result(dve, q, k, rows):
            y = y_nt[q][0:rows, :]
            dve.wait_ge(s_aff[q], k * 2 + 1)
            nc.vector.tensor_tensor(y, y, gamma_sb[0:rows, :], ALU.mult).then_inc(s_aff[q], 1)
            dve.wait_ge(s_aff[q], k * 2 + 2)
            nc.vector.tensor_tensor(y, y, x_nt[q][0:rows, :], ALU.add).then_inc(s_res[q], 1)

        @block.vector
        def _(dve):
            def statistics(i, steps, bn, mv, rows, r, data):
                if i:
                    dve.wait_ge(steps, bn_steps(i))
                for n in range(r):
                    last = nc.vector.bn_stats(bn[0:rows, n, :], data[0:rows, n, :])
                last.then_inc(steps, 1)
                dve.wait_ge(steps, bn_steps(i) + 1)
                for n in range(r):
                    last = nc.vector.bn_aggr(mv[i % 2][0:rows, n, :], bn[0:rows, n, :])
                last.then_inc(steps, 1)

            def scales(i, steps, done, std, inv, nmr, mv, rows, r):
                dve.wait_ge(std, i + 1)
                nc.vector.reciprocal(inv[0:rows, 0:r], inv[0:rows, 0:r]).then_inc(steps, 1)
                dve.wait_ge(steps, done + 1)
                nc.vector.scalar_tensor_tensor(out=nmr[0:rows, 0:r], in0=mv[i % 2][0:rows, 0:r, 0], scalar=-1.0,
                                               in1=inv[0:rows, 0:r], op0=ALU.mult, op1=ALU.mult).then_inc(steps, 1)

            def scale_chunk(i, done):
                rows, r = (REST_N, 1) if i == 0 else (P, CR)
                slot = (i - 1) % XS
                scales(i, s_bn, done, s_std, rstd[slot], nmr[slot], mv, rows, r)

            def copy_batches(first, last):
                for i in range(first, last + 1):
                    part, n, b0, nb = batches[i]
                    dve.wait_ge(s_tr, i + 1)
                    nc.vector.tensor_copy(listT[n][:, b0 * P:(b0 + nb) * P],
                                          tr_bank(i)[:, 0:nb * P]).then_inc(s_trc, 1)

            dve.wait_ge(s_xr, 16)
            statistics(0, s_bn, bn, mv, REST_N, 1, xr[:, :].rearrange("p (r d) -> p r d", r=1))
            comp_b = comp_sb[:, :, :].rearrange("p r b -> p b r")

            def coefficients(s, tiles):
                if not (isinstance(s, int) and s == 0):
                    dve.wait_ge(s_M, s * SG)
                nc.vector.tensor_tensor(typ_is[:, 0:tiles, :],
                                        typT[:, bass.ds(s * ST, tiles)].unsqueeze(2).to_broadcast([P, tiles, NR]),
                                        iota_rel[:, :].unsqueeze(1).to_broadcast([P, tiles, NR]),
                                        ALU.is_equal).then_inc(s_coef, 1)
                dve.wait_ge(s_coef, s * 3 + 1)
                for b in range(NB):
                    last = nc.vector.tensor_tensor(typ_comp[:, 0:tiles, b, :], typ_is[:, 0:tiles, :],
                                                   comp_b[:, b:b + 1, :].to_broadcast([P, tiles, NR]), ALU.mult)
                last.then_inc(s_coef, 1)
                dve.wait_ge(s_coef, s * 3 + 2)
                nc.vector.tensor_reduce(coef[:, 0:tiles, :].rearrange("p t b -> p (t b)"),
                                        typ_comp[:, 0:tiles, :, :].rearrange("p t b r -> p (t b) r"),
                                        AX, ALU.add).then_inc(s_coef, 1)

            def find_windows():
                dve.wait_ge(s_const, 7)
                dve.wait_ge(s_first, 1)
                nc.vector.tensor_tensor(dloc[:, :, :], dstT[:, 0:NT].rearrange("p (g t) -> p g t", t=GT),
                                        p_out[REST][:, 0:NG].unsqueeze(2).to_broadcast([P, NG, GT]), ALU.subtract)
                nc.vector.tensor_tensor(offs[:, :], p_out[REST][:, 0:NG], step_base[:, 0:NG], ALU.add).then_inc(s_chk, 1)
                dve.wait_ge(s_chk, 1)
                nc.vector.tensor_tensor(room[:, :], offs[:, :],
                                        least[:, :, :].rearrange("p s j -> p (s j)")[:, 0:NG],
                                        ALU.subtract).then_inc(s_chk, 1)
                nc.vector.tensor_copy(offs_i[:, :], offs[0:1, :])
                dve.wait_ge(s_chk, 2)
                flat = dloc[:, :, :].rearrange("p g t -> p (g t)")
                nc.vector.tensor_reduce(lim[:, 0:1], flat, AX, ALU.min)
                nc.vector.tensor_reduce(lim[:, 1:2], flat, AX, ALU.max)
                nc.vector.tensor_reduce(lim[:, 2:3], room[:, :], AX, ALU.min)
                nc.vector.tensor_reduce(lim[:, 3:4], offs[:, :], AX, ALU.max).then_inc(s_chk, 1)
                dve.wait_ge(s_chk, 3)
                nc.vector.tensor_scalar(okay[:, 0:1], lim[:, 0:1], 0.0, None, ALU.is_ge)
                nc.vector.tensor_scalar(okay[:, 1:2], lim[:, 1:2], float(WIN - 1), None, ALU.is_le)
                nc.vector.tensor_scalar(okay[:, 2:3], lim[:, 2:3], 0.0, None, ALU.is_ge)
                nc.vector.tensor_scalar(okay[:, 3:4], lim[:, 3:4], float(AW - WIN), None, ALU.is_le).then_inc(s_chk, 1)
                for n in range(3):
                    dve.wait_ge(s_chk, 4 + n)
                    nc.vector.tensor_tensor(okay[:, 0:1], okay[:, 0:1], okay[:, n + 1:n + 2], ALU.mult).then_inc(s_chk, 1)
                dve.wait_ge(s_chk, 7)
                nc.vector.memset(lim[:, :], 0.0).then_inc(s_chk, 1)

            def set_flag():
                dve.wait_ge(s_cnt, 1)
                nc.vector.tensor_scalar(flag_i[:, :], p_out[0][0:1, 0:1], float(P), None, ALU.is_ge).then_inc(s_flag, 1)

            for c in range(NCHUNK):
                dve.wait_ge(s_x[c % XS], 16 * (c // XS + 1))
                statistics(c + 1, s_bn, bn, mv, P, CR, xc[c % XS])
                scale_chunk(c, bn_steps(c + 1) + 2)
                if c == 1:
                    copy_batches(ends[0] + 1, ends[1])
                if c == 2:
                    find_windows()
                if c == 3:
                    copy_batches(ends[1] + 1, ends[2])
                    set_flag()
                if c == 4:
                    copy_batches(ends[2] + 1, ends[3])
                    dve.wait_ge(s_comp, 16)
                    dve.wait_ge(s_trc, len(batches) - 1)
                    coefficients(0, ST)
                    nc.vector.memset(acc[:, :, :], 0.0).then_inc(s_shift, 3)
            scale_chunk(NCHUNK, bn_steps(NCHUNK) + 4)
            dve.wait_ge(s_par, 16 * 5)
            dve.wait_ge(s_flag, 1)
            windows = dve.value_load(flag_i[0:1, 0:1], min_val=0, max_val=1)
            def make_M(s, j):
                g = s * SG + j
                if not (isinstance(s, int) and s == 0 and j == 0):
                    dve.wait_ge(s_M, g)
                nc.vector.tensor_tensor(here[:, :, :],
                                        dloc[:, bass.ds(g, 1), :].rearrange("p a t -> p (a t)")
                                        .unsqueeze(2).to_broadcast([P, GT, WIN]),
                                        iota_win[:, :].unsqueeze(1).to_broadcast([P, GT, WIN]),
                                        ALU.is_equal).then_inc(s_here, 1)
                if j == 0:
                    hold(dve, s_coef, s * 3 + 3)
                if not (isinstance(s, int) and s == 0 and j < MS):
                    hold(dve, s_agg, g - 1 if j < 2 else g - 2)
                dve.wait_ge(s_here, g + 1)
                for b in range(NB):
                    last = nc.vector.tensor_tensor(M[:, j % MS, :, b, :], here[:, :, :],
                                                   coef[:, j * GT:(j + 1) * GT, b].unsqueeze(2)
                                                   .to_broadcast([P, GT, WIN]), ALU.mult)
                last.then_inc(s_M, 1)

            def flush(s, j, off):
                g = s * SG + j
                if j == 0:
                    hold(dve, s_shift, s * 3 + 3)
                if not (isinstance(s, int) and s == 0 and j == 0):
                    hold(dve, s_flush, g)
                dve.wait_ge(s_agg, g + 1)
                window = acc[:, :, bass.ds(off, WIN)]
                nc.vector.tensor_tensor(window, window,
                                        p_sum[j % MS][:, 0:KB * WIN].rearrange("p (c w) -> p c w", c=KB),
                                        ALU.add).then_inc(s_flush, 1)

            def row_statistics(j):
                dve.wait_ge(s_gath[j], 16 * GT)
                statistics(j, s_bn_g, bn_g, mv_g, P, GT, gath[:, j, :, :])

            def row_scales(j, done):
                scales(j, s_bn_g, done, s_std_g, rstd_g[j % RS], nmr_g[j % RS], mv_g, P, GT)

            def superstep(s, groups):
                first = isinstance(s, int) and s == 0
                if not first:
                    coefficients(s, groups * GT)
                _, off = nc.values_load_multi_w_load_instructions(
                    offs_i[0:1, bass.ds(s * SG, groups)], engines=[mybir.EngineType.DVE],
                    min_val=0, max_val=AW - WIN)
                make_M(s, 0)
                if first:
                    row_statistics(0)
                    row_statistics(1)
                    row_scales(0, bn_steps(1) + 2)
                settled, apart = (SETTLED, 3) if groups == SG else (SETTLED_LAST, 1)
                for j in range(groups):
                    if j + 1 < groups:
                        make_M(s, j + 1)
                    if first and j + 2 < groups:
                        row_statistics(j + 2)
                    if first and j + 1 < groups:
                        row_scales(j + 1, bn_steps(min(j + 2, SG - 1)) + (2 if j + 2 < SG else 4))
                    if first:
                        if j:
                            flush(s, j - 1, off[j - 1])
                        if j == SG - 1:
                            flush(s, j, off[j])
                    else:
                        flush(s, j, off[j])
                    for q in range(0 if first else 2):
                        if j == settled + q * apart:
                            dve_addends(dve, q, s - 1, P)
                        if j == settled + q * apart + 1:
                            dve_sum(dve, q, s - 1, P)
                        if j == settled + q * apart + (2 if groups == SG else 1):
                            dve_norm(dve, q, s - 1, P)
                            dve_result(dve, q, s - 1, P)
                    if groups < SG and j == groups - 3:
                        dve_addends(dve, REST, 0, REST_N)
                if groups < SG:
                    return
                if not first:
                    hold(dve, s_mm[0], s)
                    hold(dve, s_mm[1], s)
                dve.wait_ge(s_flush, s * SG + SG)
                nc.vector.tensor_copy(acc[:, :, 0:STEP], acc[:, :, STEP:2 * STEP]).then_inc(s_shift, 1)
                dve.wait_ge(s_shift, s * 3 + 4)
                nc.vector.tensor_copy(acc[:, :, STEP:AW - STEP], acc[:, :, 2 * STEP:AW]).then_inc(s_shift, 1)
                dve.wait_ge(s_shift, s * 3 + 5)
                nc.vector.memset(acc[:, :, AW - STEP:AW], 0.0).then_inc(s_shift, 1)

            with dve.If(windows):
                superstep(0, SG)
                with dve.Fori(1, S_LAST) as s:
                    superstep(s, SG)
                superstep(S_LAST, LAST_G)
                dve_sum(dve, REST, 0, REST_N)
                dve_norm(dve, REST, 0, REST_N)
                dve_result(dve, REST, 0, REST_N)
            with dve.Else():
                first_rows_in(dve)
                nc.vector.memset(g_zero, 0.0).then_inc(g_zeroed, 1)
                with dve.Fori(0, NT) as k:
                    nc.vector.tensor_copy(g_dst[:, :], dstT[:, bass.ds(k, 1)])
                    nc.vector.tensor_copy(g_wide, dstT[:, bass.ds(k, 1)].to_broadcast([P, P])).then_inc(g_wid, 1)
                    nc.vector.tensor_tensor(g_ti, typT[:, bass.ds(k, 1)].to_broadcast([P, NR]), iota_rel[:, :],
                                            ALU.is_equal).then_inc(g_mk, 1)
                    dve.wait_ge(g_mk, k * 9 + 1)
                    nc.vector.tensor_tensor(g_tc, g_ti.unsqueeze(1).to_broadcast([P, NB, NR]), comp_b,
                                            ALU.mult).then_inc(g_mk, 1)
                    dve.wait_ge(g_mk, k * 9 + 2)
                    nc.vector.tensor_reduce(g_coef[:, :], g_tc, AX, ALU.add).then_inc(g_mk, 1)
                    hold(dve, g_mk, k * 9 + 3)
                    dve.wait_ge(g_tr, k + 1)
                    nc.vector.tensor_scalar(g_same, p_sum[0][:, 0:P], g_dst[:, 0:1], None,
                                            ALU.is_equal).then_inc(g_mk, 1)
                    dve.wait_ge(g_mk, k * 9 + 4)
                    nc.vector.tensor_tensor(g_prev, g_same, below[:, :], ALU.mult).then_inc(g_mk, 1)
                    dve.wait_ge(g_mk, k * 9 + 5)
                    nc.vector.tensor_reduce(g_first[:, 0:1], g_prev, AX, ALU.max)
                    nc.vector.tensor_tensor(g_first[:, 1:2], waste[:, :], g_dst[:, :], ALU.subtract).then_inc(g_mk, 1)
                    dve.wait_ge(g_mk, k * 9 + 6)
                    nc.vector.tensor_tensor(g_first[:, 0:1], g_first[:, 0:1], g_first[:, 1:2], ALU.mult).then_inc(g_mk, 1)
                    dve.wait_ge(g_mk, k * 9 + 7)
                    nc.vector.tensor_tensor(g_dst_i, g_first[:, 0:1], g_dst[:, :], ALU.add).then_inc(g_mk, 1)
                    for b in range(NB):
                        last = nc.vector.tensor_scalar(g_M[:, b, :], g_same, g_coef[:, b:b + 1], None, ALU.mult)
                    last.then_inc(g_mk, 1)
                    hold(dve, g_added, k * 16 + 16)

                def node_tile(q, k, rows):
                    dve_addends(dve, q, k, rows)
                    dve_sum(dve, q, k, rows)
                    dve_norm(dve, q, k, rows)
                    dve_result(dve, q, k, rows)

                with dve.Fori(0, NPAIR) as i:
                    for q in range(2):
                        node_tile(q, i, P)
                node_tile(REST, 0, REST_N)


_INS = ["x", "src", "dst", "edge_type_8", "L0_gnn_basis", "L0_gnn_comp", "L0_gnn_loop_w", "L0_gnn_h_bias",
        "L0_gnn_ln_gamma", "L0_gnn_ln_beta"]


def kernel(**inputs):
    import numpy as _np
    import concourse.bacc as _bacc
    from concourse import mybir as _mybir
    from concourse.bass_utils import run_bass_kernel_spmd as _run

    nc = _bacc.Bacc("TRN2", target_bir_lowering=False, num_devices=1)
    arrays, args = {}, []
    for name in _INS:
        a = _np.ascontiguousarray(inputs[name])
        arrays[f"in_{name}"] = a
        args.append(nc.dram_tensor(f"in_{name}", a.shape, _mybir.dt.from_np(a.dtype), kind="ExternalInput").ap())
    shape = inputs["x"].shape
    args.append(nc.dram_tensor("out_0", shape, _mybir.dt.from_np(_np.dtype("float32")), kind="ExternalOutput").ap())
    build_rgcn(nc, *args)
    r = _run(nc, [arrays], core_ids=[0])
    return r.results[0]["out_0"]
```

```python
from contextlib import ExitStack

import numpy as np

import concourse.bass as bass
from concourse import mybir

F32 = mybir.dt.float32
I32 = mybir.dt.int32
ALU = mybir.AluOpType
ACT = mybir.ActivationFunctionType
AX = mybir.AxisListType.X

P = 128
EPS = 1e-5


def build_rgcn(nc, x, src, dst, etype, basis, comp, loop_w, h_bias, ln_gamma, ln_beta, out):
    N, D = x.shape
    E = src.shape[0]
    NB = basis.shape[0]
    NR = comp.shape[0]
    HALVES = D // P
    KB = HALVES * NB

    GT = 6
    SG = 11
    WIN = 32
    STEP = 2 * P
    ST = SG * GT
    NG = -(-E // (GT * P))
    NT = NG * GT
    S_LAST = N // STEP
    LAST_G = NG - S_LAST * SG
    LAST_T = -(-E // P) - (NG - 1) * GT
    assert 0 < LAST_G <= SG and ST <= P
    AW = 2 * STEP + 2 * WIN
    SETTLED = 4
    SETTLED_LAST = 1
    APART = 3
    assert SETTLED_LAST == 1 and LAST_G > 3
    EB = -(-NT // P)
    FULL_T, REST_E = E // P, E % P
    MAIN_T = (FULL_T // P) * P
    REST_T = FULL_T - MAIN_T

    ROWS = N // P
    REST_N = N - ROWS * P
    CR = 6
    NCHUNK = ROWS // CR
    XS = 6
    assert ROWS % CR == 0 and NCHUNK > XS
    NPAIR = N // STEP
    assert N - NPAIR * STEP == REST_N
    AGG_ROWS = -(-(N + P) // P) * P
    DB = NB * D

    h_table = nc.dram_tensor("h_table", [N, D], F32, kind="Internal").ap()
    agg_table = nc.dram_tensor("agg_table", [AGG_ROWS, DB], F32, kind="Internal").ap()

    ctx = ExitStack()
    with ctx:
        def sb(name, shape, dt=F32):
            return ctx.enter_context(nc.sbuf_tensor(name, shape, dt))

        def ps(name, shape):
            return ctx.enter_context(nc.psum_tensor(name, shape, F32))

        def sem(name):
            return ctx.enter_context(nc.semaphore(name))

        ident = sb("ident", [P, P])
        ones = sb("ones", [P, P])
        below = sb("below", [P, P])
        iota_i = sb("iota_i", [P, (S_LAST + 1) * SG], I32)
        iota_win = sb("iota_win", [P, WIN])
        iota_rel = sb("iota_rel", [P, NR])
        waste_i = sb("waste_i", [P, 1], I32)
        waste = sb("waste", [P, 1])
        step_base = sb("step_base", [P, (S_LAST + 1) * SG])
        least = sb("least", [P, S_LAST + 1, SG])
        basis_sb = sb("basis_sb", [P, NB, HALVES, D])
        loop_sb = sb("loop_sb", [P, HALVES, D])
        comp_sb = sb("comp_sb", [P, NR, NB])
        bias_sb = sb("bias_sb", [P, D])
        gamma_sb = sb("gamma_sb", [P, D])
        beta_sb = sb("beta_sb", [P, D])

        acc = sb("acc", [P, KB, AW])
        typ_comp_mem = sb("typ_comp", [P, ST * NB * NR])
        acc_mem = acc[:, :, :].rearrange("p c n -> p (c n)")
        assert 2 * EB * P <= KB * AW
        rawf = [m.rearrange("p (b e) -> p b e", e=P) for m in (
            acc_mem[:, 0:EB * P], acc_mem[:, EB * P:2 * EB * P], typ_comp_mem[:, 0:EB * P])]
        raw = [m.bitcast(I32) for m in rawf]
        srcT = sb("srcT", [P, EB * P])
        dstT = sb("dstT", [P, EB * P])
        typT = sb("typT", [P, EB * P])
        dloc = sb("dloc", [P, NG, GT])
        room = sb("room", [P, NG])
        offs = sb("offs", [P, NG])
        offs_i = sb("offs_i", [1, NG], I32)
        lim = sb("lim", [P, 4])
        okay = sb("okay", [P, 4])
        flag_i = sb("flag_i", [1, 1], I32)

        xc = [sb(f"xc{i}", [P, CR, D]) for i in range(XS)]
        xr = sb("xr", [REST_N, D])
        bn = sb("bn", [P, CR, 6])
        mv = [sb(f"mv{i}", [P, CR, 2]) for i in range(2)]
        eps_sb = sb("eps_sb", [P, 1])
        rstd = [sb(f"rstd{i}", [P, CR]) for i in range(XS)]
        nmr = [sb(f"nmr{i}", [P, CR]) for i in range(XS)]

        bn_g = sb("bn_g", [P, GT, 6])
        mv_g = [sb(f"mv_g{i}", [P, GT, 2]) for i in range(2)]
        RS = 3
        rstd_g = [sb(f"rstd_g{i}", [P, GT]) for i in range(RS)]
        nmr_g = [sb(f"nmr_g{i}", [P, GT]) for i in range(RS)]

        src_now = sb("src_now", [P, ST], I32)
        gath = sb("gath", [P, SG, GT, D])
        typ_is = sb("typ_is", [P, ST, NR])
        typ_comp = typ_comp_mem[:, :].rearrange("p (t b r) -> p t b r", b=NB, r=NR)
        here = sb("here", [P, GT, WIN])
        MS = 3
        M = sb("M", [P, MS, GT, NB, WIN])

        SLOTS = range(3)
        REST = 2
        PAIR = ((0, P), (1, P))
        LAST_TILES = PAIR + ((REST, REST_N),)
        x_nt = [sb(f"x_nt{q}", [P, D]) for q in SLOTS]
        h_nt = [sb(f"h_nt{q}", [P, D]) for q in SLOTS]
        hT_nt = [sb(f"hT_nt{q}", [P, HALVES, P]) for q in SLOTS]
        z_nt = [sb(f"z_nt{q}", [P, D]) for q in SLOTS]
        bn_nt = [sb(f"bn_nt{q}", [P, 6]) for q in SLOTS]
        mv_nt = [sb(f"mv_nt{q}", [P, 2]) for q in SLOTS]
        rstd_nt = [sb(f"rstd_nt{q}", [P, 1]) for q in SLOTS]
        nmr_nt = [sb(f"nmr_nt{q}", [P, 1]) for q in SLOTS]
        y_nt = [sb(f"y_nt{q}", [P, D]) for q in SLOTS]

        g_src = src_now[:, 0:1]
        g_dst_i = src_now[:, 1:2]
        g_dst = sb("g_dst", [P, 1])
        g_first = sb("g_first", [P, 2])
        g_coef = sb("g_coef", [P, NB])
        g_tc = typ_comp[:, 0, :, :]
        g_ti = typ_is[:, 0, :]
        g_rows = gath[:, 0, 0, :]
        g_wide = gath[:, 1, 0, 0:P]
        g_same = gath[:, 1, 1, 0:P]
        g_prev = gath[:, 1, 2, 0:P]
        g_M = gath[:, 2, 0:2, :].rearrange("p t (a e) -> p (t a) e", a=2)
        g_sums = gath[:, 3, 0:NB, :].rearrange("p t d -> p (t d)")
        g_zero = gath[:, 4, 0:NB, :].rearrange("p t d -> p (t d)")
        agg_nt = [gath[:, 5 + q, 0:NB, :].rearrange("p t d -> p (t d)") for q in SLOTS]
        aggT_nt = [gath[:, 8 + q, 0:NB, :].rearrange("p t d -> p (t d)") for q in SLOTS]

        p_sum = [ps(f"p_sum{i}", [P, 512]) for i in range(MS)]
        p_out = [ps(f"p_out{q}", [P, 512]) for q in SLOTS]
        p_wide = ps("p_wide", [P, 1024])

        w_gamma, w_beta = p_wide[:, 0:D], p_wide[:, D:2 * D]
        at = 512
        w_coef = p_wide[:, at:at + ST * NB].rearrange("p (t b) -> p t b", b=NB)
        at += ST * NB
        w_win = p_wide[:, at:at + WIN]
        at += WIN
        w_rel = p_wide[:, at:at + NR]
        at += NR
        w_comp = p_wide[:, at:at + NR * NB].rearrange("p (b r) -> p b r", r=NR)
        assert 2 * D <= 512 and at + NR * NB <= 1024

        s_const = sem("s_const")
        s_comp = sem("s_comp")
        s_par = sem("s_par")
        s_src0 = sem("s_src0")
        s_raw = [sem(f"s_raw{n}") for n in range(3)]
        s_pad = sem("s_pad")
        s_flt = sem("s_flt")
        s_tr = sem("s_tr")
        s_trc0 = sem("s_trc0")
        s_trc = sem("s_trc")
        s_x = [sem(f"s_x{i}") for i in range(XS)]
        s_xr = sem("s_xr")
        s_bn = sem("s_bn")
        s_eps = sem("s_eps")
        s_std = sem("s_std")
        s_h = sem("s_h")
        s_hd = [sem(f"s_hd{i}") for i in range(XS)]
        s_hr = sem("s_hr")
        s_first = sem("s_first")
        s_chk = sem("s_chk")
        s_cnt = sem("s_cnt")
        s_flag = sem("s_flag")
        held = sem("held")

        s_stage = sem("s_stage")
        s_gath = [sem(f"s_gath{j}") for j in range(SG)]
        s_bn_g = sem("s_bn_g")
        s_std_g = sem("s_std_g")
        s_ps = sem("s_ps")
        s_rows = sem("s_rows")
        s_coef = sem("s_coef")
        s_here = sem("s_here")
        s_M = sem("s_M")
        s_agg = sem("s_agg")
        s_flush = sem("s_flush")
        s_shift = sem("s_shift")

        s_ld = [sem(f"s_ld{q}") for q in SLOTS]
        s_hT = [sem(f"s_hT{q}") for q in SLOTS]
        s_hTc = [sem(f"s_hTc{q}") for q in SLOTS]
        s_mm = [sem(f"s_mm{q}") for q in SLOTS]
        s_z = [sem(f"s_z{q}") for q in SLOTS]
        s_gelu = [sem(f"s_gelu{q}") for q in SLOTS]
        s_nrm = [sem(f"s_nrm{q}") for q in SLOTS]
        s_aff = [sem(f"s_aff{q}") for q in SLOTS]
        s_res = [sem(f"s_res{q}") for q in SLOTS]
        s_out = [sem(f"s_out{q}") for q in SLOTS]

        g_zeroed = sem("g_zeroed")
        g_clear = sem("g_clear")
        g_staged = sem("g_staged")
        g_gath = sem("g_gath")
        g_wid = sem("g_wid")
        g_tr = sem("g_tr")
        g_mk = sem("g_mk")
        g_mm = sem("g_mm")
        g_copied = sem("g_copied")
        g_added = sem("g_added")
        g_ld = [sem(f"g_ld{q}") for q in SLOTS]
        g_aT = sem("g_aT")
        g_aTc = sem("g_aTc")

        block = ctx.enter_context(nc.Block())

        def hold(eng, semaphore, value):
            eng.wait_ge(semaphore, value)
            eng.sem_inc(held, 1)

        def tiles_in(groups, j):
            return LAST_T if groups < SG and j == groups - 1 else GT

        def last_of(q):
            return 0 if q == REST else S_LAST - 1

        def first_rows_in(eng):
            for j in range(SG):
                eng.wait_ge(s_gath[j], 16 * GT)

        def bn_steps(i):
            return 0 if i == 0 else 4 * i - 2

        pads = (0, N - 1, NR)

        x_rows = x[0:ROWS * P, :].rearrange("(p r) d -> p r d", p=P)
        h_rows = h_table[0:ROWS * P, :].rearrange("(p r) d -> p r d", p=P)

        SRC, DST, TYP = range(3)
        PARTS = ((SRC, 0, 1), (DST, 0, EB), (SRC, 1, EB), (TYP, 0, EB))
        G_BATCH = 4
        batches = [(part, n, b, min(G_BATCH, b1 - b)) for part, (n, b0, b1) in enumerate(PARTS)
                   for b in range(b0, b1, G_BATCH)]
        ends = [max(i for i, batch in enumerate(batches) if batch[0] == part) for part in range(len(PARTS))]
        listT = (srcT, dstT, typT)

        def tr_bank(i):
            return (p_wide[:, 0:512], p_wide[:, 512:1024], p_sum[0][:, :], p_sum[1][:, :])[i % 4]


        def sp_load_nt(sp, q, row, rows):
            sp.dma_start(x_nt[q][0:rows, :], x[bass.ds(row, rows), :]).then_inc(s_ld[q], 16)
            sp.dma_start(h_nt[q][0:rows, :], h_table[bass.ds(row, rows), :]).then_inc(s_ld[q], 16)

        def sp_store_nt(sp, q, k, row, rows):
            sp.wait_ge(s_res[q], k + 1)
            sp.dma_start(out[bass.ds(row, rows), :], y_nt[q][0:rows, :]).then_inc(s_out[q], 16)

        def sp_node_tiles(sp, k, row, tiles, sums=None):
            for i, (q, rows) in enumerate(tiles):
                if sums is not None:
                    sums(q, row + i * P, rows)
                sp_load_nt(sp, q, row + i * P, rows)
            for i, (q, rows) in enumerate(tiles):
                sp_store_nt(sp, q, k, row + i * P, rows)
            for q, rows in tiles:
                hold(sp, s_out[q], k * 16 + 16)

        @block.sync
        def _(sp):
            def load_list(n, a, b0):
                sp.dma_start(raw[n][:, b0:MAIN_T // P, :],
                             a[b0 * P * P:MAIN_T * P].rearrange("(b t e) -> t b e", t=P, e=P)).then_inc(s_raw[n], 16)
                sp.wait_ge(s_pad, n + 1)
                if REST_T:
                    sp.dma_start(raw[n][0:REST_T, EB - 1, :],
                                 a[MAIN_T * P:FULL_T * P].rearrange("(t e) -> t e", e=P)).then_inc(s_raw[n], 16)
                if REST_E:
                    sp.dma_start(raw[n][REST_T:REST_T + 1, EB - 1, 0:REST_E],
                                 a[FULL_T * P:E].rearrange("(t e) -> t e", t=1)).then_inc(s_raw[n], 16)

            def load_x(c):
                if c >= XS:
                    sp.wait_ge(s_hd[c % XS], 16 * (c // XS))
                sp.dma_start(xc[c % XS][:, :, :], x_rows[:, c * CR:(c + 1) * CR, :]).then_inc(s_x[c % XS], 16)

            sp.dma_start(raw[SRC][:, 0, :], src[0:P * P].rearrange("(t e) -> t e", e=P)).then_inc(s_src0, 16)
            sp.dma_start(xr[:, :], x[ROWS * P:N, :]).then_inc(s_xr, 16)
            load_x(0)
            load_list(DST, dst, 0)
            load_x(1)
            load_x(2)
            load_list(SRC, src, 1)
            load_list(TYP, etype, 0)
            sp.dma_start(comp_sb[:, :, :].rearrange("p r b -> p (r b)"),
                         comp.rearrange("r b -> (r b)").partition_broadcast(P)).then_inc(s_comp, 16)
            for c in range(3, NCHUNK):
                load_x(c)
            for to, what in ((basis_sb[:, :, :, :], basis.rearrange("b (h p) o -> p b h o", p=P)),
                             (loop_sb[:, :, :], loop_w.rearrange("(h p) o -> p h o", p=P)),
                             (bias_sb[:, :], h_bias.partition_broadcast(P)),
                             (gamma_sb[:, :], ln_gamma.partition_broadcast(P)),
                             (beta_sb[:, :], ln_beta.partition_broadcast(P))):
                sp.dma_start(to, what).then_inc(s_par, 16)

            sp.wait_ge(s_flag, 1)
            windows = sp.value_load(flag_i[0:1, 0:1], min_val=0, max_val=1)
            for i in range(XS):
                sp.wait_ge(s_hd[i], 16 * len(range(i, NCHUNK, XS)))
            sp.wait_ge(s_hr, 16)
            with sp.If(windows):
                sp_load_nt(sp, REST, NPAIR * STEP, REST_N)
                with sp.Fori(1, S_LAST) as s:
                    sp_node_tiles(sp, s - 1, s * STEP - STEP, PAIR)
                sp_node_tiles(sp, S_LAST - 1, (S_LAST - 1) * STEP, PAIR)
                sp_store_nt(sp, REST, 0, NPAIR * STEP, REST_N)
            with sp.Else():
                sp.wait_ge(g_zeroed, 1)
                sp.dma_start(agg_table.rearrange("(j p) c -> p j c", p=P),
                             g_zero.unsqueeze(1).to_broadcast([P, AGG_ROWS // P, DB])).then_inc(g_clear, 16)
                sp.wait_ge(g_added, 16 * NT)

                def load_sums(q, row, rows):
                    sp.dma_start(agg_nt[q][0:rows, :], agg_table[bass.ds(row, rows), :]).then_inc(g_ld[q], 16)

                with sp.Fori(0, NPAIR) as i:
                    sp_node_tiles(sp, i, i * STEP, PAIR, load_sums)
                sp_node_tiles(sp, 0, NPAIR * STEP, ((REST, REST_N),), load_sums)
            sp.wait_ge(s_out[0], 16 * NPAIR)
            sp.wait_ge(s_out[1], 16 * NPAIR)
            sp.wait_ge(s_out[REST], 16)


        @block.gpsimd
        def _(pool):
            pool.memset(ident[:, :], 0.0).then_inc(s_const, 1)
            pool.memset(ones[:, :], 1.0).then_inc(s_const, 1)
            pool.wait_ge(s_const, 2)
            pool.affine_select(out=ident[:, :], in_=ident[:, :], compare_op=ALU.not_equal, fill=1.0,
                               base=0, pattern=[[-1, P]], channel_multiplier=1).then_inc(s_const, 1)
            pool.memset(eps_sb[:, :], EPS).then_inc(s_eps, 1)
            for n in (DST, SRC, TYP):
                pool.memset(raw[n][:, EB - 1, :], pads[n]).then_inc(s_pad, 1)
            pool.affine_select(out=below[:, :], in_=ones[:, :], compare_op=ALU.is_gt, fill=0.0,
                               base=0, pattern=[[-1, P]], channel_multiplier=1)
            pool.iota(iota_i[:, 0:WIN], pattern=[[1, WIN]], base=0, channel_multiplier=0)
            pool.iota(waste_i[:, :], pattern=[[0, 1]], base=N, channel_multiplier=1).then_inc(s_const, 1)
            pool.wait_ge(s_const, 4)
            pool.tensor_copy(iota_win[:, :], iota_i[:, 0:WIN])
            pool.tensor_copy(iota_rel[:, :], iota_i[:, 0:NR])
            pool.tensor_copy(waste[:, :], waste_i[:, :]).then_inc(s_const, 1)
            pool.wait_ge(s_const, 5)
            pool.iota(iota_i[:, :], pattern=[[-STEP, S_LAST + 1], [0, SG]], base=STEP, channel_multiplier=0)
            pool.memset(least[:, :, 0:SETTLED_LAST], 0.0)
            pool.memset(least[:, 0:S_LAST, SETTLED_LAST:SETTLED], 0.0)
            pool.memset(least[:, S_LAST, SETTLED_LAST:SG], float(STEP))
            pool.memset(least[:, 0:S_LAST, SETTLED:SG], float(STEP)).then_inc(s_const, 1)

            def gather(table, to, index, semaphore):
                pool.indirect_dma_start(to, None, table,
                                        bass.IndirectOffsetOnAxis(ap=index, axis=0)).then_inc(semaphore, 16)

            pool.wait_ge(s_stage, 2)
            for j in range(SG):
                for t in range(GT):
                    gather(x, gath[:, j, t, :], src_now[:, j * GT + t:j * GT + t + 1], s_gath[j])

            pool.wait_ge(s_flag, 1)
            windows = pool.value_load(flag_i[0:1, 0:1], min_val=0, max_val=1)
            for i in range(XS):
                pool.wait_ge(s_hd[i], 16 * len(range(i, NCHUNK, XS)))
            pool.wait_ge(s_hr, 16)

            def superstep(s, groups):
                for j in range(groups):
                    hold(pool, s_agg, (s - 1) * SG + j + 1)
                    if j == 0 or j == GT:
                        hold(pool, s_stage, s * 2 + (1 if j == 0 else 2))
                    for t in range(tiles_in(groups, j)):
                        gather(h_table, gath[:, j, t, :], src_now[:, j * GT + t:j * GT + t + 1], s_gath[j])

            with pool.If(windows):
                with pool.Fori(1, S_LAST) as s:
                    superstep(s, SG)
                superstep(S_LAST, LAST_G)
            with pool.Else():
                first_rows_in(pool)
                pool.wait_ge(g_clear, 16)
                with pool.Fori(0, NT) as k:
                    hold(pool, g_staged, k + 1)
                    gather(h_table, g_rows, g_src, g_gath)
                    hold(pool, g_copied, k + 1)
                    pool.indirect_dma_start(
                        agg_table, bass.IndirectOffsetOnAxis(ap=g_dst_i, axis=0), g_sums, None,
                        compute_op=ALU.add).then_inc(g_added, 16)


        def pe_transpose_h(pe, q, k, rows):
            hold(pe, s_ld[q], (k + 1) * 32)
            for half in range(HALVES):
                last = nc.tensor.transpose(p_out[q][:, D + half * P:D + half * P + rows],
                                           h_nt[q][0:rows, half * P:(half + 1) * P], ident[0:rows, 0:rows])
            last.then_inc(s_hT[q], 1)

        def pe_node_tile_h(pe, q, k, rows):
            hold(pe, s_hTc[q], k + 1)
            nc.tensor.matmul(p_out[q][0:rows, 0:D], ones[0:1, 0:rows], bias_sb[0:1, :], start=True, stop=False)
            for half in range(HALVES):
                nc.tensor.matmul(p_out[q][0:rows, 0:D], hT_nt[q][:, half, 0:rows], loop_sb[:, half, :],
                                 start=False, stop=False)

        def pe_node_tile_sums(pe, q, rows, sums):
            for half in range(HALVES):
                for b in range(NB):
                    last = nc.tensor.matmul(p_out[q][0:rows, 0:D], sums(half, b), basis_sb[:, b, half, :],
                                            start=False, stop=(half == HALVES - 1 and b == NB - 1))
            last.then_inc(s_mm[q], 1)

        @block.tensor
        def _(pe):
            pe.wait_ge(s_const, 3)
            for i, (part, n, b0, nb) in enumerate(batches):
                pe.wait_ge(s_flt, part + 1)
                if i == 4:
                    pe.wait_ge(s_trc0, 1)
                if i > 4:
                    pe.wait_ge(s_trc, i - 4)
                for b in range(nb):
                    last = nc.tensor.transpose(tr_bank(i)[:, b * P:(b + 1) * P], rawf[n][:, b0 + b, :], ident[:, :])
                last.then_inc(s_tr, 1)
                if i == ends[1] + 1:
                    pe.wait_ge(s_trc, ends[1])
                    nc.tensor.matmul(p_out[REST][:, 0:NG], ones[0:1, :],
                                     dstT[0:1, 0:NT].rearrange("p (g t) -> p g t", t=GT)[:, :, 0],
                                     start=True, stop=True).then_inc(s_first, 1)
                if i == ends[2]:
                    pe.wait_ge(s_chk, 7)
                    nc.tensor.matmul(p_out[0][0:1, 0:1], okay[:, 0:1], ones[:, 0:1], start=True, stop=True).then_inc(s_cnt, 1)

            pe.wait_ge(s_flag, 1)
            windows = pe.value_load(flag_i[0:1, 0:1], min_val=0, max_val=1)
            pe.wait_ge(s_par, 16 * 5)

            def acc_tile(at, rows):
                return lambda half, b: acc[:, half * NB + b, at:at + rows]

            def group(s, j, tiles):
                g = s * SG + j
                if isinstance(s, int) and s == 0:
                    pe.wait_ge(s_rows, j + 1)
                else:
                    hold(pe, s_gath[j], s * (16 * GT) + 16 * tiles)
                free = g - 1 if j < 2 else g - 2
                if not (isinstance(s, int) and s == 0 and j < MS):
                    hold(pe, s_flush, free)
                pe.wait_ge(s_M, g + 1)
                for half in range(HALVES):
                    for t in range(tiles):
                        last = nc.tensor.matmul(p_sum[j % MS][:, half * P:(half + 1) * P],
                                                gath[:, j, t, half * P:(half + 1) * P],
                                                M[:, j % MS, t, :, :].rearrange("p b w -> p (b w)"),
                                                start=(t == 0), stop=(t == tiles - 1))
                last.then_inc(s_agg, 1)

            def superstep(s, groups):
                first = isinstance(s, int) and s == 0
                for j in range(groups):
                    group(s, j, tiles_in(groups, j))
                    if groups < SG and j == 0:
                        for q, rows in LAST_TILES:
                            pe_transpose_h(pe, q, last_of(q), rows)
                    for q in range(0 if first or groups < SG else 2):
                        if j == SETTLED + q * APART - 1:
                            pe_transpose_h(pe, q, s - 1, P)
                        if j == SETTLED + q * APART:
                            pe_node_tile_h(pe, q, s - 1, P)
                            hold(pe, s_flush, s * SG + SETTLED)
                            pe_node_tile_sums(pe, q, P, acc_tile(q * P, P))
                    if groups < SG and j < len(LAST_TILES):
                        q, rows = LAST_TILES[j]
                        pe_node_tile_h(pe, q, last_of(q), rows)
                        if q != REST:
                            hold(pe, s_flush, s * SG + SETTLED_LAST)
                            pe_node_tile_sums(pe, q, rows, acc_tile(q * P, rows))

            with pe.If(windows):
                superstep(0, SG)
                with pe.Fori(1, S_LAST) as s:
                    superstep(s, SG)
                superstep(S_LAST, LAST_G)
                pe.wait_ge(s_flush, NG)
                pe_node_tile_sums(pe, REST, REST_N, acc_tile(STEP, REST_N))
            with pe.Else():
                with pe.Fori(0, NT) as k:
                    pe.wait_ge(g_wid, k + 1)
                    nc.tensor.transpose(p_sum[0][:, 0:P], g_wide, ident[:, :]).then_inc(g_tr, 1)
                    hold(pe, g_gath, k * 16 + 16)
                    pe.wait_ge(g_mk, k * 9 + 9)
                    for b in range(NB):
                        last = nc.tensor.matmul(p_wide[:, b * D:(b + 1) * D], g_M[:, b, :], g_rows,
                                                start=True, stop=True)
                    last.then_inc(g_mm, 1)

                def node_tile(q, k, n, rows):
                    pe_transpose_h(pe, q, k, rows)
                    hold(pe, g_ld[q], k * 16 + 16)
                    for c in range(KB):
                        last = nc.tensor.transpose(p_wide[:, c * P:c * P + rows],
                                                   agg_nt[q][0:rows, c * P:(c + 1) * P], ident[0:rows, 0:rows])
                    last.then_inc(g_aT, 1)
                    hold(pe, g_aTc, n + 1)
                    pe_node_tile_h(pe, q, k, rows)
                    pe_node_tile_sums(pe, q, rows, lambda half, b: aggT_nt[q][
                        :, (b * HALVES + half) * P:(b * HALVES + half) * P + rows])

                pe.wait_ge(g_copied, NT)
                with pe.Fori(0, NPAIR) as i:
                    for q in range(2):
                        node_tile(q, i, i * 2 + q, P)
                node_tile(REST, 0, 2 * NPAIR, REST_N)


        def act_copy_h(act, q, k, rows):
            act.wait_ge(s_hT[q], k + 1)
            nc.scalar.copy(hT_nt[q][:, :, 0:rows],
                           p_out[q][:, D:2 * D].rearrange("p (h r) -> p h r", h=HALVES)[:, :, 0:rows]
                           ).then_inc(s_hTc[q], 1)

        def act_gelu(act, q, k, rows):
            act.wait_ge(s_z[q], k * 2 + 1)
            nc.scalar.activation(z_nt[q][0:rows, :], z_nt[q][0:rows, :], ACT.Gelu).then_inc(s_gelu[q], 1)
            act.wait_ge(s_nrm[q], k * 5 + 2)
            nc.scalar.activation(rstd_nt[q][0:rows, :], mv_nt[q][0:rows, 1:2], ACT.Sqrt,
                                 bias=eps_sb[0:rows, :]).then_inc(s_nrm[q], 1)

        def act_affine(act, q, k, rows):
            act.wait_ge(s_nrm[q], k * 5 + 5)
            nc.scalar.activation(y_nt[q][0:rows, :], z_nt[q][0:rows, :], ACT.Identity,
                                 bias=nmr_nt[q][0:rows, :], scale=rstd_nt[q][0:rows, :]).then_inc(s_aff[q], 1)

        @block.scalar
        def _(act):
            def relu_chunk(buf, rows, r, slot, done):
                for i in range(r):
                    last = nc.scalar.activation(buf[0:rows, i, :], buf[0:rows, i, :], ACT.Relu,
                                                bias=nmr[slot][0:rows, i:i + 1], scale=rstd[slot][0:rows, i:i + 1])
                last.then_inc(s_h, 1)
                act.wait_ge(s_h, done)

            def as_float(part):
                n, b0, b1 = PARTS[part]
                if part == 0:
                    act.wait_ge(s_src0, 16)
                else:
                    act.wait_ge(s_raw[n], 16 * (1 + bool(REST_T) + bool(REST_E)))
                nc.scalar.copy(rawf[n][:, b0:b1, :], raw[n][:, b0:b1, :]).then_inc(s_flt, 1)

            def std_chunk(i):
                rows, r = (REST_N, 1) if i == 0 else (P, CR)
                act.wait_ge(s_bn, bn_steps(i) + 2)
                nc.scalar.activation(rstd[(i - 1) % XS][0:rows, 0:r], mv[i % 2][0:rows, 0:r, 1], ACT.Sqrt,
                                     bias=eps_sb[0:rows, :]).then_inc(s_std, 1)

            as_float(0)
            act.wait_ge(s_tr, 1)
            nc.scalar.copy(src_now[:, :], tr_bank(0)[:, 0:ST]).then_inc(s_stage, 2)
            nc.scalar.copy(srcT[:, 0:P], tr_bank(0)[:, 0:P]).then_inc(s_trc0, 1)
            act.wait_ge(s_eps, 1)
            std_chunk(0)
            for i in range(NCHUNK + 1):
                if i < NCHUNK:
                    std_chunk(i + 1)
                    act.wait_ge(s_bn, bn_steps(i + 1) + 4)
                else:
                    act.wait_ge(s_bn, bn_steps(i) + 6)
                if i == 0:
                    relu_chunk(xr[:, :].rearrange("p (r d) -> p r d", r=1), REST_N, 1, XS - 1, 1)
                    act.dma_start(h_table[ROWS * P:N, :], xr[:, :]).then_inc(s_hr, 16)
                else:
                    slot = (i - 1) % XS
                    relu_chunk(xc[slot], P, CR, slot, i + 1)
                    act.dma_start(h_rows[:, (i - 1) * CR:i * CR, :], xc[slot][:, :, :]).then_inc(s_hd[slot], 16)
                if i < 3:
                    as_float(i + 1)

            def std_group(j):
                if j >= RS:
                    act.wait_ge(s_rows, j - RS + 1)
                act.wait_ge(s_bn_g, bn_steps(j) + 2)
                nc.scalar.activation(rstd_g[j % RS][:, :], mv_g[j % 2][:, :, 1], ACT.Sqrt,
                                     bias=eps_sb[:, :]).then_inc(s_std_g, 1)

            act.wait_ge(s_trc, ends[2])
            nc.scalar.activation(acc[:, :, :].rearrange("p c n -> p (c n)"), ones[:, 0:1].to_broadcast([P, KB * AW]),
                                 ACT.Copy, scale=0.0).then_inc(s_shift, 3)
            std_group(0)
            std_group(1)
            act.wait_ge(s_flag, 1)
            windows = act.value_load(flag_i[0:1, 0:1], min_val=0, max_val=1)

            def stage(s, j0, j1):
                c0, n = j0 * GT, (j1 - j0) * GT
                nc.scalar.copy(src_now[:, c0:c0 + n], srcT[:, bass.ds(s * ST + c0, n)]).then_inc(s_stage, 1)

            def shift(s):
                if not (isinstance(s, int) and s == 0):
                    hold(act, s_mm[0], s)
                    hold(act, s_mm[1], s)
                act.wait_ge(s_flush, s * SG + SG)
                nc.scalar.copy(acc[:, :, 0:STEP], acc[:, :, STEP:2 * STEP]).then_inc(s_shift, 1)
                act.wait_ge(s_shift, s * 3 + 4)
                nc.scalar.copy(acc[:, :, STEP:AW - STEP], acc[:, :, 2 * STEP:AW]).then_inc(s_shift, 1)

            def superstep(s, after):
                for j in range(GT):
                    hold(act, s_gath[j], (s + 1) * (16 * GT))
                stage(s + 1, 0, min(GT, after))
                act_copy_h(act, 0, s - 1, P)
                act_gelu(act, 0, s - 1, P)
                act_affine(act, 0, s - 1, P)
                act_copy_h(act, 1, s - 1, P)
                act_gelu(act, 1, s - 1, P)
                act_affine(act, 1, s - 1, P)
                if after > GT:
                    for j in range(GT, SG):
                        hold(act, s_gath[j], (s + 1) * (16 * GT))
                    stage(s + 1, GT, after)
                shift(s)

            def first_superstep():
                for j in range(GT):
                    act.wait_ge(s_gath[j], 16 * GT)
                stage(1, 0, GT)
                for j in range(SG):
                    if j + 1 < SG:
                        if j:
                            std_group(j + 1)
                        act.wait_ge(s_bn_g, bn_steps(j + 1) + 4)
                    else:
                        act.wait_ge(s_bn_g, bn_steps(j) + 6)
                    for t in range(GT):
                        last = nc.scalar.activation(gath[:, j, t, :], gath[:, j, t, :], ACT.Relu,
                                                    bias=nmr_g[j % RS][:, t:t + 1], scale=rstd_g[j % RS][:, t:t + 1])
                    last.then_inc(s_rows, 1)
                    if j == GT:
                        for i in range(GT, SG):
                            act.wait_ge(s_gath[i], 16 * GT)
                        stage(1, GT, SG)

            with act.If(windows):
                first_superstep()
                shift(0)
                with act.Fori(1, S_LAST - 1) as s:
                    superstep(s, SG)
                superstep(S_LAST - 1, LAST_G)
                for q, rows in LAST_TILES:
                    act_copy_h(act, q, last_of(q), rows)
                for q, rows in LAST_TILES:
                    act_gelu(act, q, last_of(q), rows)
                    act_affine(act, q, last_of(q), rows)
            with act.Else():
                first_rows_in(act)
                nc.scalar.copy(g_src, srcT[:, 0:1]).then_inc(g_staged, 1)
                with act.Fori(0, NT) as k:
                    act.wait_ge(g_mm, k + 1)
                    for i in range(2):
                        last = nc.scalar.copy(g_sums[:, i * 512:(i + 1) * 512], p_wide[:, i * 512:(i + 1) * 512])
                    last.then_inc(g_copied, 1)
                    nc.scalar.copy(g_src, srcT[:, bass.ds(k + 1, 1)]).then_inc(g_staged, 1)

                def node_tile(q, k, n, rows):
                    act_copy_h(act, q, k, rows)
                    act.wait_ge(g_aT, n + 1)
                    nc.scalar.copy(aggT_nt[q].rearrange("p (c r) -> p c r", c=KB)[:, :, 0:rows],
                                   p_wide[:, :].rearrange("p (c r) -> p c r", c=KB)[:, :, 0:rows]).then_inc(g_aTc, 1)
                    act_gelu(act, q, k, rows)
                    act_affine(act, q, k, rows)

                with act.Fori(0, NPAIR) as i:
                    for q in range(2):
                        node_tile(q, i, i * 2 + q, P)
                node_tile(REST, 0, 2 * NPAIR, REST_N)


        def dve_sum(dve, q, k, rows, beta):
            hold(dve, s_ld[q], k * 32 + 32)
            dve.wait_ge(s_mm[q], k + 1)
            nc.vector.tensor_tensor(z_nt[q][0:rows, :], p_out[q][0:rows, 0:D], h_nt[q][0:rows, :],
                                    ALU.add).then_inc(s_z[q], 1)
            nc.vector.tensor_tensor(p_out[q][0:rows, D:2 * D], x_nt[q][0:rows, :], beta[0:rows, :],
                                    ALU.add).then_inc(s_z[q], 1)

        def dve_norm(dve, q, k, rows):
            dve.wait_ge(s_gelu[q], k + 1)
            nc.vector.bn_stats(bn_nt[q][0:rows, :], z_nt[q][0:rows, :]).then_inc(s_nrm[q], 1)
            hold(dve, s_nrm[q], k * 5 + 1)
            nc.vector.bn_aggr(mv_nt[q][0:rows, :], bn_nt[q][0:rows, :]).then_inc(s_nrm[q], 1)
            dve.wait_ge(s_nrm[q], k * 5 + 3)
            nc.vector.reciprocal(rstd_nt[q][0:rows, :], rstd_nt[q][0:rows, :]).then_inc(s_nrm[q], 1)
            dve.wait_ge(s_nrm[q], k * 5 + 4)
            nc.vector.scalar_tensor_tensor(out=nmr_nt[q][0:rows, :], in0=mv_nt[q][0:rows, 0:1], scalar=-1.0,
                                           in1=rstd_nt[q][0:rows, :], op0=ALU.mult, op1=ALU.mult
                                           ).then_inc(s_nrm[q], 1)

        def dve_result(dve, q, k, rows, gamma):
            y = y_nt[q][0:rows, :]
            dve.wait_ge(s_aff[q], k * 2 + 1)
            nc.vector.tensor_tensor(y, y, gamma[0:rows, :], ALU.mult).then_inc(s_aff[q], 1)
            hold(dve, s_z[q], k * 2 + 2)
            dve.wait_ge(s_aff[q], k * 2 + 2)
            nc.vector.tensor_tensor(y, y, p_out[q][0:rows, D:2 * D], ALU.add).then_inc(s_res[q], 1)

        @block.vector
        def _(dve):
            def statistics(i, steps, bn, mv, rows, r, data):
                if i:
                    dve.wait_ge(steps, bn_steps(i))
                for n in range(r):
                    last = nc.vector.bn_stats(bn[0:rows, n, :], data[0:rows, n, :])
                last.then_inc(steps, 1)
                dve.wait_ge(steps, bn_steps(i) + 1)
                for n in range(r):
                    last = nc.vector.bn_aggr(mv[i % 2][0:rows, n, :], bn[0:rows, n, :])
                last.then_inc(steps, 1)

            def scales(i, steps, done, std, inv, nmr, mv, rows, r):
                dve.wait_ge(std, i + 1)
                nc.vector.reciprocal(inv[0:rows, 0:r], inv[0:rows, 0:r]).then_inc(steps, 1)
                dve.wait_ge(steps, done + 1)
                nc.vector.scalar_tensor_tensor(out=nmr[0:rows, 0:r], in0=mv[i % 2][0:rows, 0:r, 0], scalar=-1.0,
                                               in1=inv[0:rows, 0:r], op0=ALU.mult, op1=ALU.mult).then_inc(steps, 1)

            def scale_chunk(i, done):
                rows, r = (REST_N, 1) if i == 0 else (P, CR)
                slot = (i - 1) % XS
                scales(i, s_bn, done, s_std, rstd[slot], nmr[slot], mv, rows, r)

            def copy_batches(first, last):
                for i in range(first, last + 1):
                    part, n, b0, nb = batches[i]
                    dve.wait_ge(s_tr, i + 1)
                    nc.vector.tensor_copy(listT[n][:, b0 * P:(b0 + nb) * P],
                                          tr_bank(i)[:, 0:nb * P]).then_inc(s_trc, 1)

            dve.wait_ge(s_xr, 16)
            statistics(0, s_bn, bn, mv, REST_N, 1, xr[:, :].rearrange("p (r d) -> p r d", r=1))
            dve.wait_ge(s_const, 6)
            nc.vector.tensor_copy(step_base[:, :], iota_i[:, :]).then_inc(s_const, 1)
            comp_b = comp_sb[:, :, :].rearrange("p r b -> p b r")

            def coefficients(s):
                if not (isinstance(s, int) and s == 0):
                    dve.wait_ge(s_M, s * SG)
                nc.vector.tensor_tensor(typ_is[:, 0:ST, :],
                                        typT[:, bass.ds(s * ST, ST)].unsqueeze(2).to_broadcast([P, ST, NR]),
                                        w_rel.unsqueeze(1).to_broadcast([P, ST, NR]),
                                        ALU.is_equal).then_inc(s_coef, 1)
                dve.wait_ge(s_coef, s * 3 + 1)
                for b in range(NB):
                    last = nc.vector.tensor_tensor(typ_comp[:, 0:ST, b, :], typ_is[:, 0:ST, :],
                                                   w_comp[:, b:b + 1, :].to_broadcast([P, ST, NR]), ALU.mult)
                last.then_inc(s_coef, 1)
                dve.wait_ge(s_coef, s * 3 + 2)
                nc.vector.tensor_reduce(w_coef.rearrange("p t b -> p (t b)"),
                                        typ_comp[:, 0:ST, :, :].rearrange("p t b r -> p (t b) r"),
                                        AX, ALU.add).then_inc(s_coef, 1)

            def make_M(s, j):
                g = s * SG + j
                if not (isinstance(s, int) and s == 0 and j == 0):
                    dve.wait_ge(s_M, g)
                nc.vector.tensor_tensor(here[:, :, :],
                                        dloc[:, bass.ds(g, 1), :].rearrange("p a t -> p (a t)")
                                        .unsqueeze(2).to_broadcast([P, GT, WIN]),
                                        w_win.unsqueeze(1).to_broadcast([P, GT, WIN]),
                                        ALU.is_equal).then_inc(s_here, 1)
                if j == 0:
                    hold(dve, s_coef, s * 3 + 3)
                if not (isinstance(s, int) and s == 0 and j < MS):
                    hold(dve, s_agg, g - 1 if j < 2 else g - 2)
                dve.wait_ge(s_here, g + 1)
                for b in range(NB):
                    last = nc.vector.tensor_tensor(M[:, j % MS, :, b, :], here[:, :, :],
                                                   w_coef[:, j * GT:(j + 1) * GT, b].unsqueeze(2)
                                                   .to_broadcast([P, GT, WIN]), ALU.mult)
                last.then_inc(s_M, 1)

            def row_statistics(j):
                dve.wait_ge(s_gath[j], 16 * GT)
                statistics(j, s_bn_g, bn_g, mv_g, P, GT, gath[:, j, :, :])

            def row_scales(j, done):
                scales(j, s_bn_g, done, s_std_g, rstd_g[j % RS], nmr_g[j % RS], mv_g, P, GT)

            def find_windows():
                dve.wait_ge(s_const, 7)
                dve.wait_ge(s_first, 1)
                nc.vector.tensor_tensor(dloc[:, :, :], dstT[:, 0:NT].rearrange("p (g t) -> p g t", t=GT),
                                        p_out[REST][:, 0:NG].unsqueeze(2).to_broadcast([P, NG, GT]), ALU.subtract)
                nc.vector.tensor_tensor(offs[:, :], p_out[REST][:, 0:NG], step_base[:, 0:NG], ALU.add).then_inc(s_chk, 1)
                dve.wait_ge(s_chk, 1)
                nc.vector.tensor_tensor(room[:, :], offs[:, :],
                                        least[:, :, :].rearrange("p s j -> p (s j)")[:, 0:NG],
                                        ALU.subtract).then_inc(s_chk, 1)
                nc.vector.tensor_copy(offs_i[:, :], offs[0:1, :])
                dve.wait_ge(s_chk, 2)
                flat = dloc[:, :, :].rearrange("p g t -> p (g t)")
                nc.vector.tensor_reduce(lim[:, 0:1], flat, AX, ALU.min)
                nc.vector.tensor_reduce(lim[:, 1:2], flat, AX, ALU.max)
                nc.vector.tensor_reduce(lim[:, 2:3], room[:, :], AX, ALU.min)
                nc.vector.tensor_reduce(lim[:, 3:4], offs[:, :], AX, ALU.max).then_inc(s_chk, 1)
                dve.wait_ge(s_chk, 3)
                nc.vector.tensor_scalar(okay[:, 0:1], lim[:, 0:1], 0.0, None, ALU.is_ge)
                nc.vector.tensor_scalar(okay[:, 1:2], lim[:, 1:2], float(WIN - 1), None, ALU.is_le)
                nc.vector.tensor_scalar(okay[:, 2:3], lim[:, 2:3], 0.0, None, ALU.is_ge)
                nc.vector.tensor_scalar(okay[:, 3:4], lim[:, 3:4], float(AW - WIN), None, ALU.is_le).then_inc(s_chk, 1)
                for n in range(3):
                    dve.wait_ge(s_chk, 4 + n)
                    nc.vector.tensor_tensor(okay[:, 0:1], okay[:, 0:1], okay[:, n + 1:n + 2], ALU.mult).then_inc(s_chk, 1)

            def set_flag():
                dve.wait_ge(s_cnt, 1)
                nc.vector.tensor_scalar(flag_i[:, :], p_out[0][0:1, 0:1], float(P), None, ALU.is_ge).then_inc(s_flag, 1)

            for c in range(NCHUNK):
                dve.wait_ge(s_x[c % XS], 16 * (c // XS + 1))
                statistics(c + 1, s_bn, bn, mv, P, CR, xc[c % XS])
                scale_chunk(c, bn_steps(c + 1) + 2)
                if c == 1:
                    copy_batches(ends[0] + 1, ends[1])
                if c == 2:
                    find_windows()
                if c == 3:
                    copy_batches(ends[1] + 1, ends[2])
                    set_flag()
                if c == 5:
                    copy_batches(ends[2] + 1, ends[3])
            scale_chunk(NCHUNK, bn_steps(NCHUNK) + 4)
            dve.wait_ge(s_comp, 16)
            dve.wait_ge(s_trc, len(batches) - 1)
            for to, what in ((w_win, iota_win[:, :]), (w_rel, iota_rel[:, :]), (w_comp, comp_b)):
                nc.vector.tensor_copy(to, what).then_inc(s_ps, 1)
            dve.wait_ge(s_ps, 3)
            coefficients(0)
            make_M(0, 0)
            row_statistics(0)
            row_statistics(1)
            row_scales(0, bn_steps(1) + 2)
            make_M(0, 1)
            dve.wait_ge(s_par, 16 * 5)
            for to, what in ((w_gamma, gamma_sb[:, :]), (w_beta, beta_sb[:, :])):
                nc.vector.tensor_copy(to, what).then_inc(s_ps, 1)
            dve.wait_ge(s_ps, 5)
            row_statistics(2)
            row_scales(1, bn_steps(2) + 2)
            dve.wait_ge(s_flag, 1)
            windows = dve.value_load(flag_i[0:1, 0:1], min_val=0, max_val=1)

            def flush(s, j, off):
                g = s * SG + j
                if j == 0:
                    hold(dve, s_shift, s * 3 + 3)
                if not (isinstance(s, int) and s == 0 and j == 0):
                    hold(dve, s_flush, g)
                dve.wait_ge(s_agg, g + 1)
                window = acc[:, :, bass.ds(off, WIN)]
                nc.vector.tensor_tensor(window, window,
                                        p_sum[j % MS][:, 0:KB * WIN].rearrange("p (c w) -> p c w", c=KB),
                                        ALU.add).then_inc(s_flush, 1)

            def superstep(s, groups):
                first = isinstance(s, int) and s == 0
                _, off = nc.values_load_multi_w_load_instructions(
                    offs_i[0:1, bass.ds(s * SG, groups)], engines=[mybir.EngineType.DVE],
                    min_val=0, max_val=AW - WIN)
                for j in range(groups):
                    if first and 0 < j:
                        if j + 2 < SG:
                            row_statistics(j + 2)
                        if j + 1 < SG:
                            row_scales(j + 1, bn_steps(min(j + 2, SG - 1)) + (2 if j + 2 < SG else 4))
                        flush(s, j - 1, off[j - 1])
                    if j + 2 < groups:
                        make_M(s, j + 2)
                    elif groups == SG and j == SG - 2:
                        coefficients(s + 1)
                    if first and j == SG - 1:
                        make_M(s + 1, 0)
                        flush(s, j, off[j])
                    if not first:
                        flush(s, j, off[j])
                        if groups == SG and j == SG - 2:
                            make_M(s + 1, 0)
                    if groups == SG and j == SG - 1:
                        make_M(s + 1, 1)
                    for q in range(0 if first or groups < SG else 2):
                        if j == SETTLED + q * APART + 1:
                            dve_sum(dve, q, s - 1, P, w_beta)
                        if j == SETTLED + q * APART + 2:
                            dve_norm(dve, q, s - 1, P)
                            dve_result(dve, q, s - 1, P, w_gamma)
                    if groups < SG and j in (1, 2):
                        dve_sum(dve, j - 1, s - 1, P, w_beta)
                        dve_norm(dve, j - 1, s - 1, P)
                        dve_result(dve, j - 1, s - 1, P, w_gamma)
                if groups < SG:
                    return
                dve.wait_ge(s_shift, s * 3 + 5)
                nc.vector.memset(acc[:, :, AW - STEP:AW], 0.0).then_inc(s_shift, 1)

            with dve.If(windows):
                superstep(0, SG)
                with dve.Fori(1, S_LAST) as s:
                    superstep(s, SG)
                superstep(S_LAST, LAST_G)
                dve_sum(dve, REST, 0, REST_N, w_beta)
                dve_norm(dve, REST, 0, REST_N)
                dve_result(dve, REST, 0, REST_N, w_gamma)
            with dve.Else():
                first_rows_in(dve)
                nc.vector.memset(g_zero, 0.0).then_inc(g_zeroed, 1)
                with dve.Fori(0, NT) as k:
                    nc.vector.tensor_copy(g_dst[:, :], dstT[:, bass.ds(k, 1)])
                    nc.vector.tensor_copy(g_wide, dstT[:, bass.ds(k, 1)].to_broadcast([P, P])).then_inc(g_wid, 1)
                    nc.vector.tensor_tensor(g_ti, typT[:, bass.ds(k, 1)].to_broadcast([P, NR]), iota_rel[:, :],
                                            ALU.is_equal).then_inc(g_mk, 1)
                    dve.wait_ge(g_mk, k * 9 + 1)
                    nc.vector.tensor_tensor(g_tc, g_ti.unsqueeze(1).to_broadcast([P, NB, NR]), comp_b,
                                            ALU.mult).then_inc(g_mk, 1)
                    dve.wait_ge(g_mk, k * 9 + 2)
                    nc.vector.tensor_reduce(g_coef[:, :], g_tc, AX, ALU.add).then_inc(g_mk, 1)
                    hold(dve, g_mk, k * 9 + 3)
                    dve.wait_ge(g_tr, k + 1)
                    nc.vector.tensor_scalar(g_same, p_sum[0][:, 0:P], g_dst[:, 0:1], None,
                                            ALU.is_equal).then_inc(g_mk, 1)
                    dve.wait_ge(g_mk, k * 9 + 4)
                    nc.vector.tensor_tensor(g_prev, g_same, below[:, :], ALU.mult).then_inc(g_mk, 1)
                    dve.wait_ge(g_mk, k * 9 + 5)
                    nc.vector.tensor_reduce(g_first[:, 0:1], g_prev, AX, ALU.max)
                    nc.vector.tensor_tensor(g_first[:, 1:2], waste[:, :], g_dst[:, :], ALU.subtract).then_inc(g_mk, 1)
                    dve.wait_ge(g_mk, k * 9 + 6)
                    nc.vector.tensor_tensor(g_first[:, 0:1], g_first[:, 0:1], g_first[:, 1:2], ALU.mult).then_inc(g_mk, 1)
                    dve.wait_ge(g_mk, k * 9 + 7)
                    nc.vector.tensor_tensor(g_dst_i, g_first[:, 0:1], g_dst[:, :], ALU.add).then_inc(g_mk, 1)
                    for b in range(NB):
                        last = nc.vector.tensor_scalar(g_M[:, b, :], g_same, g_coef[:, b:b + 1], None, ALU.mult)
                    last.then_inc(g_mk, 1)
                    hold(dve, g_added, k * 16 + 16)

                def node_tile(q, k, rows):
                    dve_sum(dve, q, k, rows, beta_sb)
                    dve_norm(dve, q, k, rows)
                    dve_result(dve, q, k, rows, gamma_sb)

                with dve.Fori(0, NPAIR) as i:
                    for q in range(2):
                        node_tile(q, i, P)
                node_tile(REST, 0, REST_N)


_INS = ["x", "src", "dst", "edge_type_8", "L0_gnn_basis", "L0_gnn_comp", "L0_gnn_loop_w", "L0_gnn_h_bias",
        "L0_gnn_ln_gamma", "L0_gnn_ln_beta"]


def kernel(**inputs):
    import numpy as _np
    import concourse.bacc as _bacc
    from concourse import mybir as _mybir
    from concourse.bass_utils import run_bass_kernel_spmd as _run

    nc = _bacc.Bacc("TRN2", target_bir_lowering=False, num_devices=1)
    arrays, args = {}, []
    for name in _INS:
        a = _np.ascontiguousarray(inputs[name])
        arrays[f"in_{name}"] = a
        args.append(nc.dram_tensor(f"in_{name}", a.shape, _mybir.dt.from_np(a.dtype), kind="ExternalInput").ap())
    shape = inputs["x"].shape
    args.append(nc.dram_tensor("out_0", shape, _mybir.dt.from_np(_np.dtype("float32")), kind="ExternalOutput").ap())
    build_rgcn(nc, *args)
    r = _run(nc, [arrays], core_ids=[0])
    return r.results[0]["out_0"]
```
